# Optimizing a Trainium2 kernel written in Bass

```python
import numpy as np
import jax
import jax.numpy as jnp

def _softmax(x, axis=-1):
    return jax.nn.softmax(x, axis=axis)

def _gelu(x):
    return jax.nn.gelu(x, approximate=True)

def _silu(x):
    return jax.nn.silu(x)

def _sigmoid(x):
    return jax.nn.sigmoid(x)

def _layernorm(x, axis=-1, eps=1e-05):
    m = jnp.mean(x, axis=axis, keepdims=True)
    v = jnp.var(x, axis=axis, keepdims=True)
    return (x - m) / jnp.sqrt(v + eps)

def _scatter_add(tgt, idx, src, axis=0):
    return tgt.at[idx].add(src)

def _segment_sum(src, seg, n):
    return jax.ops.segment_sum(src, seg, n)
kernel_name = 'mk_macaron_d1_jaxref_r8_813a41'

def setup_inputs(seed: int=0):
    np.random.seed(seed)
    _w = jnp.asarray

    def _L0_attn_setup():
        import jax, jax.numpy as jnp
        import numpy as np
        HIDDEN = 128
        HEADS = 16
        HEAD_DIM = HIDDEN // HEADS
        B, S = (4, 256)
        key = jax.random.key(seed)
        ks = jax.random.split(key, 10)
        scale = 1.0 / np.sqrt(HIDDEN)

        def lin(k):
            return jax.random.uniform(k, (HIDDEN, HIDDEN), jnp.float32, -scale, scale)
        return {'x': jax.random.normal(ks[0], (B, S, HIDDEN), jnp.float32), 'Wq': lin(ks[1]), 'bq': jnp.zeros((HIDDEN,), jnp.float32), 'Wk': lin(ks[2]), 'bk': jnp.zeros((HIDDEN,), jnp.float32), 'Wv': lin(ks[3]), 'bv': jnp.zeros((HIDDEN,), jnp.float32), 'Wo': lin(ks[4]), 'bo': jnp.zeros((HIDDEN,), jnp.float32), 'head_mask': jnp.ones((HEADS,), jnp.float32)}
    _L0_attn_in = _L0_attn_setup()

    def _L0_ffn_setup():
        import jax, jax.numpy as jnp
        import numpy as np
        B, S, D = (1, 256, 128)
        E, K, F = (8, 2, 176)
        NS = 2
        SCALE = 2.5

        def _swiglu_mlp(x, wg, wu, wd):
            return jax.nn.silu(x @ wg) * (x @ wu) @ wd
        key = jax.random.key(seed)
        ks = jax.random.split(key, 8)
        s = 0.02
        return {'hidden_states': jax.random.normal(ks[0], (B, S, D), jnp.float32), 'gate_w': jax.random.normal(ks[1], (E, D), jnp.float32) * s, 'w_gate': jax.random.normal(ks[2], (E, D, F), jnp.float32) * s, 'w_up': jax.random.normal(ks[3], (E, D, F), jnp.float32) * s, 'w_down': jax.random.normal(ks[4], (E, F, D), jnp.float32) * s, 'sw_gate': jax.random.normal(ks[5], (D, F * NS), jnp.float32) * s, 'sw_up': jax.random.normal(ks[6], (D, F * NS), jnp.float32) * s, 'sw_down': jax.random.normal(ks[7], (F * NS, D), jnp.float32) * s}
    _L0_ffn_in = _L0_ffn_setup()
    _d = {'L0_attn_x': _L0_attn_in['x'], 'L0_attn_Wq': _L0_attn_in['Wq'], 'L0_attn_bq': _L0_attn_in['bq'], 'L0_attn_Wk': _L0_attn_in['Wk'], 'L0_attn_bk': _L0_attn_in['bk'], 'L0_attn_Wv': _L0_attn_in['Wv'], 'L0_attn_bv': _L0_attn_in['bv'], 'L0_attn_Wo': _L0_attn_in['Wo'], 'L0_attn_bo': _L0_attn_in['bo'], 'L0_attn_head_mask': _L0_attn_in['head_mask'], 'L0_ffn_gate_w': _L0_ffn_in['gate_w'], 'L0_ffn_w_gate': _L0_ffn_in['w_gate'], 'L0_ffn_w_up': _L0_ffn_in['w_up'], 'L0_ffn_w_down': _L0_ffn_in['w_down'], 'L0_ffn_sw_gate': _L0_ffn_in['sw_gate'], 'L0_ffn_sw_up': _L0_ffn_in['sw_up'], 'L0_ffn_sw_down': _L0_ffn_in['sw_down']}
    _x0 = _d['L0_attn_x']
    _d['L0_attn_x'] = jax.random.normal(jax.random.fold_in(jax.random.key(seed), 1), (16, 512, 128), dtype=_x0.dtype)
    del _x0
    return _d

def reference(L0_attn_x, L0_attn_Wq, L0_attn_bq, L0_attn_Wk, L0_attn_bk, L0_attn_Wv, L0_attn_bv, L0_attn_Wo, L0_attn_bo, L0_attn_head_mask, L0_ffn_gate_w, L0_ffn_w_gate, L0_ffn_w_up, L0_ffn_w_down, L0_ffn_sw_gate, L0_ffn_sw_up, L0_ffn_sw_down):

    def _L0_attn_ref(x, Wq, bq, Wk, bk, Wv, bv, Wo, bo, head_mask):
        import jax, jax.numpy as jnp
        import numpy as np
        HIDDEN = 128
        HEADS = 16
        HEAD_DIM = HIDDEN // HEADS
        B, S = (4, 256)
        b, s, _ = x.shape
        q = (x @ Wq.T + bq).reshape(b, s, HEADS, HEAD_DIM)
        k = (x @ Wk.T + bk).reshape(b, s, HEADS, HEAD_DIM)
        v = (x @ Wv.T + bv).reshape(b, s, HEADS, HEAD_DIM)
        attn = jnp.einsum('bqhd,bkhd->bhqk', q, k) / np.sqrt(HEAD_DIM).astype(np.float32)
        attn = jax.nn.softmax(attn, axis=-1)
        attn = attn * head_mask[None, :, None, None]
        out = jnp.einsum('bhqk,bkhd->bqhd', attn, v).reshape(b, s, HIDDEN)
        return out @ Wo.T + bo

    def _L0_ffn_ref(hidden_states, gate_w, w_gate, w_up, w_down, sw_gate, sw_up, sw_down):
        import jax, jax.numpy as jnp
        import numpy as np
        B, S, D = (1, 256, 128)
        E, K, F = (8, 2, 176)
        NS = 2
        SCALE = 2.5

        def _swiglu_mlp(x, wg, wu, wd):
            return jax.nn.silu(x @ wg) * (x @ wu) @ wd
        identity = hidden_states
        x = hidden_states.reshape(-1, hidden_states.shape[-1])
        T = x.shape[0]
        logits = x.astype(jnp.float32) @ gate_w.astype(jnp.float32).T
        scores = jax.nn.softmax(logits, axis=-1)
        topk_w, topk_i = jax.lax.top_k(scores, K)
        topk_w = topk_w / (topk_w.sum(-1, keepdims=True) + 1e-20) * SCALE
        combine = jnp.zeros((T, E), jnp.float32).at[jnp.arange(T)[:, None], topk_i].set(topk_w)
        g = jax.nn.silu(jnp.einsum('td,edf->etf', x, w_gate)) * jnp.einsum('td,edf->etf', x, w_up)
        expert_out = jnp.einsum('etf,efd->etd', g, w_down)
        y = jnp.einsum('te,etd->td', combine, expert_out).astype(x.dtype)
        y = y.reshape(identity.shape)
        return y + _swiglu_mlp(identity, sw_gate, sw_up, sw_down)
    x = L0_attn_x
    x = x + 0.5 * _L0_ffn_ref(_layernorm(x, axis=-1), L0_ffn_gate_w, L0_ffn_w_gate, L0_ffn_w_up, L0_ffn_w_down, L0_ffn_sw_gate, L0_ffn_sw_up, L0_ffn_sw_down)
    x = x + _L0_attn_ref(_layernorm(x, axis=-1), L0_attn_Wq, L0_attn_bq, L0_attn_Wk, L0_attn_bk, L0_attn_Wv, L0_attn_bv, L0_attn_Wo, L0_attn_bo, L0_attn_head_mask)
    x = x + 0.5 * _L0_ffn_ref(_layernorm(x, axis=-1), L0_ffn_gate_w, L0_ffn_w_gate, L0_ffn_w_up, L0_ffn_w_down, L0_ffn_sw_gate, L0_ffn_sw_up, L0_ffn_sw_down)
    return x

_drawn_inputs = setup_inputs


def setup_inputs(seed=0):
    import zlib

    import numpy as np

    out = dict(_drawn_inputs(seed))
    spreads = {'L0_attn_bq': (0.0, 0.8),
     'L0_attn_bk': (0.0, 0.8),
     'L0_attn_bv': (0.0, 0.1),
     'L0_attn_bo': (0.0, 0.1)}
    factors = {'L0_attn_Wq': 5.166,
     'L0_attn_Wk': 5.061,
     'L0_attn_Wv': 3.099,
     'L0_ffn_gate_w': 5.436,
     'L0_ffn_w_gate': 4.739,
     'L0_ffn_w_up': 4.699,
     'L0_ffn_w_down': 4.7,
     'L0_ffn_sw_gate': 5.903,
     'L0_ffn_sw_up': 5.89,
     'L0_ffn_sw_down': 5.904}
    for name, (base, spread) in spreads.items():
        noise = np.random.default_rng([zlib.crc32(name.encode()), seed]).standard_normal(out[name].shape)
        drawn = base * np.exp(spread * noise) if base else spread * noise
        out[name] = jnp.asarray(drawn.astype(out[name].dtype))
    for name, factor in factors.items():
        out[name] = (out[name] * factor).astype(out[name].dtype)
    return out
```

```python
import concourse.bass as bass
from concourse import mybir
from contextlib import ExitStack

F32 = mybir.dt.float32
F32R = mybir.dt.float32r
BF16 = mybir.dt.bfloat16
ALU = mybir.AluOpType
ACT = mybir.ActivationFunctionType
AX = mybir.AxisListType

P = 128
D = 128
E, F, FS = 8, 176, 352
ROUTED, HID = E * F, E * F + FS
TILES = -(-HID // P)
RTILES = ROUTED // P
S = 512
NT = S // P
NB = 16
PARTS = 3
HEADS, HD = 16, 8
EPS = 1e-5
TOPK_EPS = 1e-20
SCALE = 2.5
assert ROUTED % P == 0


def width(f):
    return min(P, HID - f * P)


class Turn:

    def __init__(self, j, k):
        self.j, self.k, self.par = j, k, k % 2

    def count(self, per, more=0):
        const = self.k * per + more
        return const if isinstance(self.j, int) else self.j * (2 * per) + const

    def half(self, per, more=0):
        const = (self.k // 2) * per + more
        return const if isinstance(self.j, int) else self.j * per + const

    def step(self, n):
        return Turn(self.j, self.k + n)

    def of(self, dram):
        return dram[self.k] if isinstance(self.j, int) else dram[self.j * 2 + self.k]


def need(eng, sem, value):
    if isinstance(value, int) and value <= 0:
        return
    eng.wait_ge(sem, value)


def all_batches(eng, batch):
    batch(Turn(0, 0), True, False)
    batch(Turn(0, 1), False, False)
    with eng.Fori(0, (NB - 4) // 2) as j:
        for k in (2, 3):
            batch(Turn(j, k), False, False)
    batch(Turn(0, NB - 2), False, False)
    batch(Turn(0, NB - 1), False, True)


def split(nc, eng, sem, high, low, full, base):
    nc.vector.tensor_copy(high, full).then_inc(sem, 1)
    eng.wait_ge(sem, base + 1)
    nc.vector.tensor_tensor(low, full, high.bitcast(F32), ALU.subtract).then_inc(sem, 1)


def setup(nc, dram, w):
    with ExitStack() as ctx:
        sb = lambda name, shape: ctx.enter_context(nc.sbuf_tensor(name, shape, F32))
        sem = lambda name: ctx.enter_context(nc.semaphore(name))
        gate, up = sb("gate_full", [P, HID]), sb("up_full", [P, HID])
        down = sb("down_full", [P, TILES, D])
        wq, wk = sb("wq_full", [P, D]), sb("wk_full", [P, D])
        selector = sb("selector_full", [PARTS * E, ROUTED])
        gate_loaded, up_loaded, down_loaded = sem("gate_loaded"), sem("up_loaded"), sem("down_loaded")
        attn_loaded, consts_loaded, done = sem("attn_loaded"), sem("consts_loaded"), sem("setup_done")
        block = ctx.enter_context(nc.Block())
        full_rows = HID // P * P

        @block.sync
        def _(sp):
            for dst, routed, shared, loaded in ((gate, dram["w_gate"], dram["sw_gate"], gate_loaded),
                                                (up, dram["w_up"], dram["sw_up"], up_loaded)):
                sp.dma_start(dst[:, 0:ROUTED].rearrange("d (e f) -> d e f", e=E),
                             routed.rearrange("e d f -> d e f")).then_inc(loaded, 16)
                sp.dma_start(dst[:, ROUTED:HID], shared).then_inc(loaded, 16)

        @block.scalar
        def _(act):
            act.dma_start(down[:, 0:RTILES, :],
                          dram["w_down"].rearrange("e f d -> (e f) d").rearrange("(t p) d -> p t d", p=P)
                          ).then_inc(down_loaded, 16)
            act.dma_start(down[:, RTILES:TILES - 1, :],
                          dram["sw_down"][0:full_rows - ROUTED, :].rearrange("(t p) d -> p t d", p=P)
                          ).then_inc(down_loaded, 16)
            act.dma_start(down[0:width(TILES - 1), TILES - 1, :],
                          dram["sw_down"][full_rows - ROUTED:FS, :]).then_inc(down_loaded, 16)
            act.dma_start(w.gate_w[:], dram["gate_w_t"]).then_inc(consts_loaded, 16)
            act.dma_start(w.ident[:], dram["identity"]).then_inc(consts_loaded, 16)
            act.dma_start(w.rank[:], dram["rank"]).then_inc(consts_loaded, 16)
            act.dma_start(selector[:], dram["selector"]).then_inc(consts_loaded, 16)
            act.dma_start(wq[:], dram["wq_t"]).then_inc(attn_loaded, 16)
            act.dma_start(wk[:], dram["wk_t"]).then_inc(attn_loaded, 16)
            act.dma_start(w.wv[:], dram["wv_t"]).then_inc(attn_loaded, 16)
            act.dma_start(w.wo[:], dram["wo_t"]).then_inc(attn_loaded, 16)
            act.dma_start(w.bq[:], dram["bq"].rearrange("(p a) -> p a", a=1)).then_inc(attn_loaded, 16)
            act.dma_start(w.bk[:], dram["bk"].rearrange("(p a) -> p a", a=1)).then_inc(attn_loaded, 16)
            for dst, name in ((w.bv, "bv"), (w.bo, "bo"), (w.head_mask, "head_mask")):
                act.dma_start(dst[:], dram[name].rearrange("(a n) -> a n", a=1)
                              .to_broadcast([P, dram[name].shape[0]])).then_inc(attn_loaded, 16)

        @block.vector
        def _(dve):
            nc.vector.memset(w.minus_half[:], -0.5).then_inc(done, 1)
            nc.vector.memset(w.selector[:], 0.0).then_inc(done, 1)
            dve.wait_ge(done, 2)
            dve.wait_ge(consts_loaded, 64)
            nc.vector.tensor_copy(w.ident16[:], w.ident[:]).then_inc(done, 1)
            nc.vector.tensor_copy(w.selector[0:PARTS * E, :], selector[:]).then_inc(done, 1)
            dve.wait_ge(gate_loaded, 32)
            split(nc, dve, done, w.gate[0][:], w.gate[1][:], gate[:], 4)
            dve.wait_ge(up_loaded, 32)
            split(nc, dve, done, w.up[0][:], w.up[1][:], up[:], 6)
            dve.wait_ge(down_loaded, 48)
            last = width(TILES - 1)
            split(nc, dve, done, w.down[0][:, 0:TILES - 1, :], w.down[1][:, 0:TILES - 1, :],
                  down[:, 0:TILES - 1, :], 8)
            split(nc, dve, done, w.down[0][0:last, TILES - 1, :], w.down[1][0:last, TILES - 1, :],
                  down[0:last, TILES - 1, :], 10)
            dve.wait_ge(attn_loaded, 16 * 9)
            split(nc, dve, done, w.wq[0][:], w.wq[1][:], wq[:], 12)
            split(nc, dve, done, w.wk[0][:], w.wk[1][:], wk[:], 14)
            dve.wait_ge(done, 16)


class NormBuffers:

    def __init__(self, sb):
        self.stats = sb("stats", [P, NT, 6])
        self.mean_sum, self.mean_diff, self.m2 = sb("mean_sum", [P, NT]), sb("mean_diff", [P, NT]), sb("m2", [P, NT])
        self.mean, self.diff2, self.var_within = sb("mean", [P, NT]), sb("diff2", [P, NT]), sb("var_within", [P, NT])
        self.var_eps, self.rstd = sb("var_eps", [P, NT]), sb("rstd", [P, NT])


def normalisation(nc, dve, x_in, xn, n, x_in_loaded, stats_done, var_ready, rstd_ready, normed, xn_turned):
    V = nc.vector
    STEPS = 3

    def norm_stats(b):
        dve.wait_ge(x_in_loaded[b.par], b.half(16, 16))
        for t in range(NT):
            last = V.bn_stats(n.stats[:, t, :], x_in[b.par][:, t, :])
        last.then_inc(stats_done, 1)

    def norm_var(b):
        even_mean, even_m2, odd_mean, odd_m2 = (n.stats[:, :, i] for i in (1, 2, 4, 5))
        dve.wait_ge(stats_done, b.count(STEPS, 1))
        V.tensor_tensor(n.mean_sum[:], even_mean, odd_mean, ALU.add)
        V.tensor_tensor(n.mean_diff[:], even_mean, odd_mean, ALU.subtract)
        V.tensor_tensor(n.m2[:], even_m2, odd_m2, ALU.add).then_inc(stats_done, 1)
        dve.wait_ge(stats_done, b.count(STEPS, 2))
        V.tensor_scalar(n.mean[:], n.mean_sum[:], 0.5, None, ALU.mult)
        V.scalar_tensor_tensor(n.diff2[:], n.mean_diff[:], 0.25, n.mean_diff[:], ALU.mult, ALU.mult)
        V.tensor_scalar(n.var_within[:], n.m2[:], 1.0 / D, EPS, ALU.mult, ALU.add).then_inc(stats_done, 1)
        dve.wait_ge(stats_done, b.count(STEPS, 3))
        need(dve, rstd_ready, b.count(1))
        V.tensor_tensor(n.var_eps[:], n.diff2[:], n.var_within[:], ALU.add).then_inc(var_ready, 1)

    def norm_apply(b):
        dve.wait_ge(rstd_ready, b.count(1, 1))
        need(dve, xn_turned, b.count(1))
        for t in range(NT):
            last = V.tensor_scalar(xn[:, t, :], x_in[b.par][:, t, :], n.mean[:, t:t + 1],
                                   n.rstd[:, t:t + 1], ALU.subtract, ALU.mult)
        last.then_inc(normed, 1)

    return norm_stats, norm_var, norm_apply


def ffn(nc, name, w, src, dst):
    LAG = 2
    RING = 4
    with ExitStack() as ctx:
        sb = lambda n, shape, dt=F32: ctx.enter_context(nc.sbuf_tensor(f"{name}_{n}", shape, dt))
        pb = lambda n, shape=(P, S): ctx.enter_context(nc.psum_tensor(f"{name}_{n}", list(shape), F32))
        sem = lambda n: ctx.enter_context(nc.semaphore(f"{name}_{n}"))
        pair = lambda make, n, *a: [make(f"{n}{i}", *a) for i in range(2)]

        x_in = pair(sb, "x_in", [P, NT, D])
        x_res = pair(sb, "x_res", [P, NT, D])
        x_out = pair(sb, "x_out", [P, NT, D])
        xn = sb("xn", [P, NT, D])
        xt = sb("xt", [P, S])
        xt_high, xt_low = pair(sb, "xt_high", [P, S], F32R), pair(sb, "xt_low", [P, S], F32R)
        norm = NormBuffers(sb)
        small = {n: sb(n, [P, NT, E]) for n in
                 ("z", "tanh", "first_ranks", "first", "z2", "is_second", "second_ranks", "second",
                  "chosen", "denominator", "exps", "inverse", "scores", "picked", "combine", "rest")}
        one = {n: sb(n, [P, NT]) for n in
               ("top", "first_rank", "top2", "second_rank", "total", "total_inv", "sum2", "sum2_eps", "sum2_inv")}
        combine_parts = sb("combine_parts", [P, NT, PARTS * E], BF16)
        combine_t = pair(sb, "combine_t", [P, S], BF16)
        silu = pair(sb, "silu", [P, S])
        gated = pair(sb, "gated", [P, S])
        hidden = [sb(f"hidden{i}", [P, S]) for i in range(RING)]
        hid_high = [sb(f"hid_high{i}", [P, S], F32R) for i in range(RING)]
        hid_low = [sb(f"hid_low{i}", [P, S], F32R) for i in range(RING)]
        yt = sb("yt", [P, S])
        p_gate, p_up = pair(pb, "p_gate"), pair(pb, "p_up")
        p_spread = pb("p_spread")
        p_y = pb("p_y")
        p_prep = pb("p_prep")
        p_final = pb("p_final")

        x_in_loaded, x_res_loaded, stored = pair(sem, "x_in_loaded"), pair(sem, "x_res_loaded"), pair(sem, "stored")
        zeroed = sem("zeroed")
        stats_done, var_ready, rstd_ready = sem("stats_done"), sem("var_ready"), sem("rstd_ready")
        normed, xn_turned, xt_copied = sem("normed"), sem("xn_turned"), sem("xt_copied")
        xt_high_ready, xt_low_ready = sem("xt_high_ready"), sem("xt_low_ready")
        logits_ready, z_ready, tanh_ready = sem("logits_ready"), sem("z_ready"), sem("tanh_ready")
        route_step = sem("route_step")
        combine_turned, combine_copied = sem("combine_turned"), sem("combine_copied")
        gate_ready, up_ready, spread_ready = sem("gate_ready"), sem("up_ready"), sem("spread_ready")
        silu_ready, gated_ready, weighted_ready = sem("silu_ready"), sem("gated_ready"), sem("weighted_ready")
        high_ready, low_ready, down_done = sem("high_ready"), sem("low_ready"), sem("down_done")
        y_copied, y_turned, out_ready = sem("y_copied"), sem("y_turned"), sem("out_ready")
        ROUTE_STEPS = 26

        src_b = src.rearrange("(b p t) d -> b p t d", p=P, t=NT)
        dst_b = dst.rearrange("(b p t) d -> b p t d", p=P, t=NT)
        slot = lambda turn, f: (turn.par * TILES + f) % RING
        assert 2 * TILES % RING == 0

        block = ctx.enter_context(nc.Block())

        @block.sync
        def _(sp):
            def load_in(b):
                need(sp, normed, b.count(1, -1))
                sp.dma_start(x_in[b.par][:], b.of(src_b)).then_inc(x_in_loaded[b.par], 16)

            def batch(b, first, last):
                if not last:
                    load_in(b.step(1))
                need(sp, out_ready, b.count(1, -1))
                sp.dma_start(x_res[b.par][:], b.of(src_b)).then_inc(x_res_loaded[b.par], 16)
                if not first:
                    store(b.step(-1))

            def store(b):
                sp.wait_ge(out_ready, b.count(1, 1))
                sp.dma_start(b.of(dst_b), x_out[b.par][:]).then_inc(stored[b.par], 16)

            load_in(Turn(0, 0))
            all_batches(sp, batch)
            store(Turn(0, NB - 1))
            for par in range(2):
                sp.wait_ge(stored[par], 16 * NB // 2)

        @block.tensor
        def _(pe):
            def three(out, weights, high, low, start, stop):
                nc.tensor.matmul(out, weights[0], high, start=start, stop=False)
                nc.tensor.matmul(out, weights[1], high, start=False, stop=False)
                return nc.tensor.matmul(out, weights[0], low, start=False, stop=stop)

            def prep_transpose(b):
                pe.wait_ge(normed, b.count(1, 1))
                need(pe, combine_copied, b.count(1))
                for t in range(NT):
                    last = nc.tensor.transpose(p_prep[:, t * P:(t + 1) * P], xn[:, t, :], w.ident[:])
                last.then_inc(xn_turned, 1)

            def prep_logits(b):
                pe.wait_ge(xt_copied, b.count(1, 1))
                for t in range(NT):
                    last = nc.tensor.matmul(p_prep[:, t * E:(t + 1) * E], xt[:, t * P:(t + 1) * P],
                                            w.gate_w[:], start=True, stop=True)
                last.then_inc(logits_ready, 1)

            def prep_combine(b):
                pe.wait_ge(route_step, b.count(ROUTE_STEPS, ROUTE_STEPS))
                out = p_prep[:].bitcast(BF16)
                for t in range(NT):
                    last = nc.tensor.transpose(out[0:PARTS * E, t * P:(t + 1) * P],
                                               combine_parts[:, t, :], w.ident16[:])
                last.then_inc(combine_turned, 1)

            def gate_up(b, f):
                n, cols = width(f), slice(f * P, f * P + width(f))
                need(pe, silu_ready, b.count(TILES, f - 1))
                three(p_gate[f % 2][0:n, :], [g[:, cols] for g in w.gate], xt_high[b.par][:], xt_low[b.par][:],
                      True, True).then_inc(gate_ready, 1)
                need(pe, gated_ready, b.count(TILES, f - 1))
                three(p_up[f % 2][0:n, :], [u[:, cols] for u in w.up], xt_high[b.par][:], xt_low[b.par][:],
                      True, True).then_inc(up_ready, 1)
                if f < RTILES:
                    need(pe, weighted_ready, b.count(RTILES, f))
                    nc.tensor.matmul(p_spread[:], w.selector[:, cols], combine_t[b.par][:],
                                     start=True, stop=True).then_inc(spread_ready, 1)

            def down(b, f):
                n, s = width(f), slot(b, f)
                pe.wait_ge(low_ready, b.count(TILES, f + 1))
                if f == 0:
                    need(pe, y_copied, b.count(1))
                three(p_y[:], [d[0:n, f, :] for d in w.down], hid_high[s][0:n, :], hid_low[s][0:n, :],
                      f == 0, f == TILES - 1).then_inc(down_done, 1)

            def final_transpose(b):
                pe.wait_ge(y_copied, b.count(1, 1))
                need(pe, out_ready, b.count(1))
                for t in range(NT):
                    last = nc.tensor.transpose(p_final[:, t * P:(t + 1) * P], yt[:, t * P:(t + 1) * P], w.ident[:])
                last.then_inc(y_turned, 1)

            def batch(b, first, last):
                pe.wait_ge(xt_low_ready, b.count(1, 1))
                pe.wait_ge(combine_copied, b.count(1, 1))
                for f in range(TILES):
                    gate_up(b, f)
                    if f >= LAG:
                        down(b, f - LAG)
                    elif not first:
                        down(b.step(-1), TILES + f - LAG)
                    if f == 3 and not first:
                        final_transpose(b.step(-1))
                    if not last:
                        if f == 5:
                            prep_transpose(b.step(1))
                        if f == 6:
                            prep_logits(b.step(1))
                        if f == 12:
                            prep_combine(b.step(1))

            pe.wait_ge(zeroed, 2)
            prep_transpose(Turn(0, 0))
            prep_logits(Turn(0, 0))
            prep_combine(Turn(0, 0))
            all_batches(pe, batch)
            end = Turn(0, NB - 1)
            for f in range(TILES - LAG, TILES):
                down(end, f)
            final_transpose(end)

        @block.scalar
        def _(act):
            def xt_copy(b):
                act.wait_ge(xn_turned, b.count(1, 1))
                need(act, logits_ready, b.count(1))
                need(act, xt_low_ready, b.count(1))
                nc.scalar.activation(xt[:], p_prep[:], ACT.Copy).then_inc(xt_copied, 1)

            def xt_split(b):
                act.wait_ge(xt_copied, b.count(1, 1))
                need(act, up_ready, b.count(TILES, -TILES))
                nc.scalar.activation(xt_high[b.par][:], xt[:], ACT.Copy).then_inc(xt_high_ready, 1)

            def tanh(b):
                act.wait_ge(z_ready, b.count(1, 1))
                nc.scalar.activation(small["tanh"][:], small["z"][:], ACT.Tanh, scale=0.5).then_inc(tanh_ready, 1)

            def combine_copy(b):
                act.wait_ge(combine_turned, b.count(1, 1))
                need(act, spread_ready, b.count(RTILES, -RTILES))
                nc.scalar.activation(combine_t[b.par][0:PARTS * E, :], p_prep[:].bitcast(BF16)[0:PARTS * E, 0:S],
                                     ACT.Copy).then_inc(combine_copied, 1)

            def silu_tile(b, f):
                n = width(f)
                act.wait_ge(gate_ready, b.count(TILES, f + 1))
                need(act, gated_ready, b.count(TILES, f - 1))
                nc.scalar.activation(silu[f % 2][0:n, :], p_gate[f % 2][0:n, :], ACT.Silu).then_inc(silu_ready, 1)

            def high_tile(b, f):
                n, s = width(f), slot(b, f)
                if f < RTILES:
                    act.wait_ge(weighted_ready, b.count(RTILES, f + 1))
                else:
                    act.wait_ge(gated_ready, b.count(TILES, f + 1))
                need(act, down_done, b.count(TILES, f + 1 - RING))
                nc.scalar.activation(hid_high[s][0:n, :], hidden[s][0:n, :], ACT.Copy).then_inc(high_ready, 1)

            def y_copy(b):
                act.wait_ge(down_done, b.count(TILES, TILES))
                need(act, y_turned, b.count(1))
                nc.scalar.activation(yt[:], p_y[:], ACT.Copy).then_inc(y_copied, 1)

            def batch(b, first, last):
                for f in range(TILES):
                    silu_tile(b, f)
                    if f > 0:
                        high_tile(b, f - 1)
                    elif not first:
                        high_tile(b.step(-1), TILES - 1)
                    if f == 2 and not first:
                        y_copy(b.step(-1))
                    if not last:
                        if f == 5:
                            xt_copy(b.step(1))
                        if f == 6:
                            xt_split(b.step(1))
                        if f == 7:
                            tanh(b.step(1))
                        if f == 12:
                            combine_copy(b.step(1))

            xt_copy(Turn(0, 0))
            xt_split(Turn(0, 0))
            tanh(Turn(0, 0))
            combine_copy(Turn(0, 0))
            all_batches(act, batch)
            high_tile(Turn(0, NB - 1), TILES - 1)
            y_copy(Turn(0, NB - 1))

        @block.gpsimd
        def _(pool):
            def rstd_batch(b):
                pool.wait_ge(var_ready, b.count(1, 1))
                need(pool, normed, b.count(1))
                nc.gpsimd.tensor_tensor(norm.rstd[:], norm.var_eps[:], w.minus_half[:], ALU.pow).then_inc(rstd_ready, 1)

            def xt_rest(b):
                pool.wait_ge(xt_high_ready, b.count(1, 1))
                nc.gpsimd.tensor_tensor(xt_low[b.par][:], xt[:], xt_high[b.par][:].bitcast(F32),
                                        ALU.subtract).then_inc(xt_low_ready, 1)

            def low_tile(b, f):
                n, s = width(f), slot(b, f)
                pool.wait_ge(high_ready, b.count(TILES, f + 1))
                nc.gpsimd.tensor_tensor(hid_low[s][0:n, :], hidden[s][0:n, :],
                                        hid_high[s][0:n, :].bitcast(F32), ALU.subtract).then_inc(low_ready, 1)

            def batch(b, first, last):
                for f in range(TILES):
                    if f > 0:
                        low_tile(b, f - 1)
                    elif not first:
                        low_tile(b.step(-1), TILES - 1)
                    if not last:
                        if f == 3:
                            rstd_batch(b.step(1))
                        if f == 7:
                            xt_rest(b.step(1))

            for par in range(2):
                nc.gpsimd.memset(combine_t[par][:], 0.0).then_inc(zeroed, 1)
            rstd_batch(Turn(0, 0))
            xt_rest(Turn(0, 0))
            all_batches(pool, batch)
            low_tile(Turn(0, NB - 1), TILES - 1)

        @block.vector
        def _(dve):
            V = nc.vector
            per_token = lambda a: a[:].unsqueeze(2).to_broadcast([P, NT, E])
            logits = p_prep[:, 0:NT * E].rearrange("p (t e) -> p t e", e=E)

            norm_stats, norm_var, norm_apply = normalisation(
                nc, dve, x_in, xn, norm, x_in_loaded, stats_done, var_ready, rstd_ready, normed, xn_turned)

            def route(b, part):
                z, rank = small["z"], w.rank
                done = [(0, 5, 11, 18)[part]]

                def step(instruction):
                    instruction.then_inc(route_step, 1)
                    done[0] += 1
                    dve.wait_ge(route_step, b.count(ROUTE_STEPS, done[0]))

                if part == 0:
                    dve.wait_ge(logits_ready, b.count(1, 1))
                    need(dve, tanh_ready, b.count(1))
                    step(V.tensor_reduce(one["top"][:], logits, AX.X, ALU.max))
                    V.tensor_tensor(z[:], logits, per_token(one["top"]), ALU.subtract).then_inc(z_ready, 1)
                    dve.wait_ge(z_ready, b.count(1, 1))
                    step(V.scalar_tensor_tensor(small["first_ranks"][:], z[:], 0.0, rank[:], ALU.is_equal, ALU.mult))
                    step(V.tensor_reduce(one["first_rank"][:], small["first_ranks"][:], AX.X, ALU.max))
                    step(V.tensor_tensor(small["first"][:], rank[:], per_token(one["first_rank"]), ALU.is_equal))
                    step(V.scalar_tensor_tensor(small["z2"][:], small["first"][:], -3e38, z[:], ALU.mult, ALU.add))
                if part == 1:
                    step(V.tensor_reduce(one["top2"][:], small["z2"][:], AX.X, ALU.max))
                    step(V.tensor_tensor(small["is_second"][:], small["z2"][:], per_token(one["top2"]), ALU.is_equal))
                    step(V.tensor_tensor(small["second_ranks"][:], small["is_second"][:], rank[:], ALU.mult))
                    step(V.tensor_reduce(one["second_rank"][:], small["second_ranks"][:], AX.X, ALU.max))
                    step(V.tensor_tensor(small["second"][:], rank[:], per_token(one["second_rank"]), ALU.is_equal))
                    step(V.tensor_tensor(small["chosen"][:], small["first"][:], small["second"][:], ALU.add))
                if part == 2:
                    dve.wait_ge(tanh_ready, b.count(1, 1))
                    step(V.tensor_scalar(small["denominator"][:], small["tanh"][:], -1.0, 1.0, ALU.mult, ALU.add))
                    step(V.reciprocal(small["inverse"][:], small["denominator"][:]))
                    step(V.scalar_tensor_tensor(small["exps"][:], small["tanh"][:], 1.0, small["inverse"][:],
                                                ALU.add, ALU.mult))
                    step(V.tensor_reduce(one["total"][:], small["exps"][:], AX.X, ALU.add))
                    step(V.reciprocal(one["total_inv"][:], one["total"][:]))
                    step(V.tensor_tensor(small["scores"][:], small["exps"][:], per_token(one["total_inv"]), ALU.mult))
                    step(V.tensor_tensor(small["picked"][:], small["scores"][:], small["chosen"][:], ALU.mult))
                if part == 3:
                    parts = [combine_parts[:, :, i * E:(i + 1) * E] for i in range(PARTS)]
                    cw, rest = small["combine"], small["rest"]
                    step(V.tensor_reduce(one["sum2"][:], small["picked"][:], AX.X, ALU.add))
                    step(V.tensor_scalar(one["sum2_eps"][:], one["sum2"][:], TOPK_EPS, None, ALU.add))
                    step(V.reciprocal(one["sum2_inv"][:], one["sum2_eps"][:]))
                    step(V.scalar_tensor_tensor(cw[:], small["picked"][:], SCALE, per_token(one["sum2_inv"]),
                                                ALU.mult, ALU.mult))
                    need(dve, combine_turned, b.count(1))
                    step(V.tensor_copy(parts[0], cw[:]))
                    step(V.tensor_tensor(rest[:], cw[:], parts[0], ALU.subtract))
                    step(V.tensor_copy(parts[1], rest[:]))
                    step(V.tensor_tensor(parts[2], rest[:], parts[1], ALU.subtract))

            def gated_tile(b, f):
                n, s = width(f), slot(b, f)
                dve.wait_ge(silu_ready, b.count(TILES, f + 1))
                dve.wait_ge(up_ready, b.count(TILES, f + 1))
                if f < RTILES:
                    out = gated[f % 2]
                else:
                    need(dve, low_ready, b.count(TILES, f + 1 - RING))
                    out = hidden[s]
                V.tensor_tensor(out[0:n, :], silu[f % 2][0:n, :], p_up[f % 2][0:n, :], ALU.mult).then_inc(gated_ready, 1)

            def weighted_tile(b, f):
                dve.wait_ge(gated_ready, b.count(TILES, f + 1))
                dve.wait_ge(spread_ready, b.count(RTILES, f + 1))
                need(dve, low_ready, b.count(TILES, f + 1 - RING))
                V.tensor_tensor(hidden[slot(b, f)][:], gated[f % 2][:], p_spread[:], ALU.mult).then_inc(weighted_ready, 1)

            def residual(b):
                dve.wait_ge(y_turned, b.count(1, 1))
                dve.wait_ge(x_res_loaded[b.par], b.half(16, 16))
                need(dve, stored[b.par], b.half(16))
                V.scalar_tensor_tensor(x_out[b.par][:], p_final[:].rearrange("p (t d) -> p t d", d=D), 0.5,
                                       x_res[b.par][:], ALU.mult, ALU.add).then_inc(out_ready, 1)

            def batch(b, first, last):
                for f in range(TILES):
                    if 0 < f <= RTILES:
                        weighted_tile(b, f - 1)
                    gated_tile(b, f)
                    if f == 4 and not first:
                        residual(b.step(-1))
                    if not last:
                        if f == 1:
                            norm_stats(b.step(1))
                        if f == 2:
                            norm_var(b.step(1))
                        if f == 4:
                            norm_apply(b.step(1))
                        if 7 <= f < 11:
                            route(b.step(1), f - 7)

            begin = Turn(0, 0)
            norm_stats(begin)
            norm_var(begin)
            norm_apply(begin)
            for part in range(4):
                route(begin, part)
            all_batches(dve, batch)
            residual(Turn(0, NB - 1))


def attention(nc, w, src, dst):
    QUAD = 4
    NQ = HEADS // QUAD
    COLS = 32
    ROWS = PARTS * PARTS * HD
    MAX_ROW = 96
    TILES_Q = QUAD * NT
    TILES_B = NQ * TILES_Q
    RING = 2 * QUAD
    PACK_DMA, MAX_DMA = 2 * PARTS * PARTS * 16, PARTS * 16
    inv_sqrt = 1.0 / HD ** 0.5
    with ExitStack() as ctx:
        sb = lambda n, shape, dt=F32: ctx.enter_context(nc.sbuf_tensor(f"attn_{n}", shape, dt))
        pb = lambda n: ctx.enter_context(nc.psum_tensor(f"attn_{n}", [P, S], F32))
        sem = lambda n: ctx.enter_context(nc.semaphore(f"attn_{n}"))
        pair = lambda make, n, *a: [make(f"{n}{i}", *a) for i in range(2)]

        x_in = pair(sb, "x_in", [P, NT, D])
        x_res = pair(sb, "x_res", [P, NT, D])
        x_bias = sb("x_bias", [P, NT, D])
        x_out = pair(sb, "x_out", [P, NT, D])
        xn = sb("xn", [P, NT, D])
        xt, xt_high, xt_low = sb("xt", [P, S]), sb("xt_high", [P, S], F32R), sb("xt_low", [P, S], F32R)
        norm = NormBuffers(sb)
        full = {o: sb(f"{o}_full", [P, S]) for o in "qk"}
        rest = {o: sb(f"{o}_rest", [P, S]) for o in "qk"}
        parts = {o: sb(f"{o}_parts", [P, PARTS, S], BF16) for o in "qk"}
        pack = {o: pair(sb, f"{o}_pack", [P, HEADS, S], BF16) for o in "qk"}
        values = pair(sb, "values", [P, NT, HEADS, COLS])
        maxima = pair(sb, "maxima", [P, P])
        max_neg, max_rest = sb("max_neg", [TILES_Q, P]), sb("max_rest", [TILES_Q, P])
        zeros = sb("zeros", [TILES_Q, P])
        max_parts = pair(sb, "max_parts", [TILES_Q, PARTS, P], BF16)
        exps = [sb(f"exps{i}", [P, S]) for i in range(RING)]
        o_raw = pair(sb, "o_raw", [P, S])
        sums_inv, sums_scale = sb("sums_inv", [P, NT, QUAD]), sb("sums_scale", [P, NT, QUAD])
        o_norm = sb("o_norm", [P, NT, D])
        ot = sb("ot", [P, S])
        p_max, p_exp = pair(pb, "p_max"), pair(pb, "p_exp")
        p_o = pair(pb, "p_o")
        p_a = pb("p_a")
        p_b = pb("p_b")

        x_in_loaded, x_res_loaded, stored = pair(sem, "x_in_loaded"), pair(sem, "x_res_loaded"), pair(sem, "stored")
        pool_init, dve_init = sem("pool_init"), sem("dve_init")
        stats_done, var_ready, rstd_ready = sem("stats_done"), sem("var_ready"), sem("rstd_ready")
        normed, xn_turned, xt_copied = sem("normed"), sem("xn_turned"), sem("xt_copied")
        xt_high_ready, xt_low_ready = sem("xt_high_ready"), sem("xt_low_ready")
        projected = {o: sem(f"{o}_projected") for o in "qkv"}
        copied = {o: sem(f"{o}_copied") for o in "qk"}
        first, second, third = ({o: sem(f"{o}_{n}") for o in "qk"} for n in ("first", "second", "third"))
        rested = {o: sem(f"{o}_rested") for o in "qk"}
        v_ready = sem("v_ready")
        packed = pair(sem, "packed")
        max_tile, max_read = sem("max_tile"), sem("max_read")
        max_turned, max_negated, max_step = sem("max_turned"), sem("max_negated"), sem("max_step")
        max_packed = pair(sem, "max_packed")
        exp_tile, exp_ready, pv_done = sem("exp_tile"), sem("exp_ready"), sem("pv_done")
        o_copied, o_turned, norm_step = sem("o_copied"), sem("o_turned"), sem("norm_step")
        norm_turned, ot_copied, out_projected = sem("norm_turned"), sem("ot_copied"), sem("out_projected")
        bias_ready, out_ready = sem("bias_ready"), sem("out_ready")
        NORM_STEPS, MAX_STEPS = 3, 4

        src_b = src.rearrange("(b p t) d -> b p t d", p=P, t=NT)
        dst_b = dst.rearrange("(b p t) d -> b p t d", p=P, t=NT)

        def there(b, n=0):
            return not isinstance(b.j, int) or b.k + n < NB

        def quad(b, g):
            return b.step(g // NQ), g % NQ

        block = ctx.enter_context(nc.Block())

        @block.sync
        def _(sp):
            def load_in(b):
                need(sp, normed, b.count(1, -1))
                sp.dma_start(x_in[b.par][:], b.of(src_b)).then_inc(x_in_loaded[b.par], 16)

            def load_res(b):
                need(sp, bias_ready, b.count(1, -1))
                sp.dma_start(x_res[b.par][:], b.of(src_b)).then_inc(x_res_loaded[b.par], 16)

            def store(b):
                sp.wait_ge(out_ready, b.count(1, 1))
                sp.dma_start(b.of(dst_b), x_out[b.par][:]).then_inc(stored[b.par], 16)

            def pack_operands(b):
                for i, sem_i in enumerate((first, second, third)):
                    sp.wait_ge(sem_i["q"], b.count(1, 1))
                    for j in range(PARTS):
                        r = (i * PARTS + j) * HD
                        sp.dma_start(pack["q"][b.par][r:r + HD, :, :], parts["q"][:, i, :])\
                            .then_inc(packed[b.par], 16)
                for j, sem_j in enumerate((first, second, third)):
                    sp.wait_ge(sem_j["k"], b.count(1, 1))
                    for i in range(PARTS):
                        r = (i * PARTS + j) * HD
                        sp.dma_start(pack["k"][b.par][r:r + HD, :, :], parts["k"][:, j, :])\
                            .then_inc(packed[b.par], 16)

            def pack_max(b, g):
                sp.wait_ge(max_step, b.count(MAX_STEPS * NQ, MAX_STEPS * (g + 1)))
                for i in range(PARTS):
                    sp.dma_start(pack["q"][b.par][MAX_ROW + i:MAX_ROW + i + 1, g * QUAD:(g + 1) * QUAD, :],
                                 max_parts[g % 2][:, i, :]).then_inc(max_packed[g % 2], 16)

            def batch(b, is_first, is_last):
                load_res(b)
                pack_max(b, 1)
                if there(b, 1):
                    pack_operands(b.step(1))
                pack_max(b, 2)
                if not is_first:
                    store(b.step(-1))
                if there(b, 2):
                    load_in(b.step(2))
                pack_max(b, 3)
                if there(b, 1):
                    pack_max(b.step(1), 0)

            begin = Turn(0, 0)
            load_in(begin)
            load_in(begin.step(1))
            sp.wait_ge(dve_init, 6)
            pack_operands(begin)
            pack_max(begin, 0)
            all_batches(sp, batch)
            store(Turn(0, NB - 1))
            for par in range(2):
                sp.wait_ge(stored[par], 16 * NB // 2)

        @block.tensor
        def _(pe):
            def turn_x(b):
                pe.wait_ge(normed, b.count(1, 1))
                need(pe, max_negated, b.count(NQ, 1 - NQ))
                for t in range(NT):
                    last = nc.tensor.transpose(p_a[:, t * P:(t + 1) * P], xn[:, t, :], w.ident[:])
                last.then_inc(xn_turned, 1)

            def project_qk(b, o, weights):
                pe.wait_ge(xt_low_ready, b.count(1, 1))
                if o == "q":
                    need(pe, max_negated, b.count(NQ, 2 - NQ))
                else:
                    pe.wait_ge(copied["q"], b.count(1, 1))
                nc.tensor.matmul(p_a[:], weights[0][:], xt_high[:], start=True, stop=False)
                nc.tensor.matmul(p_a[:], weights[1][:], xt_high[:], start=False, stop=False)
                nc.tensor.matmul(p_a[:], weights[0][:], xt_low[:], start=False, stop=True)\
                    .then_inc(projected[o], 1)

            def project_v(b):
                pe.wait_ge(copied["k"], b.count(1, 1))
                need(pe, max_negated, b.count(NQ, 3 - NQ))
                for t in range(NT):
                    last = nc.tensor.matmul(p_a[:, t * P:(t + 1) * P], xt[:, t * P:(t + 1) * P], w.wv[:],
                                            start=True, stop=True)
                last.then_inc(projected["v"], 1)

            def score_max(b, g, t, h):
                n = g * TILES_Q + t * QUAD + h
                need(pe, max_read, b.count(TILES_B, n - 1))
                nc.tensor.matmul(p_max[n % 2][:], pack["q"][b.par][0:ROWS, g * QUAD + h, t * P:(t + 1) * P],
                                 pack["k"][b.par][0:ROWS, g * QUAD + h, :], start=True, stop=True)\
                    .then_inc(max_tile, 1)

            def score_exp(b, g, t, h):
                n = g * TILES_Q + t * QUAD + h
                need(pe, exp_ready, b.count(TILES_B, n - 1))
                rows = MAX_ROW + PARTS
                nc.tensor.matmul(p_exp[n % 2][:], pack["k"][b.par][0:rows, g * QUAD + h, t * P:(t + 1) * P],
                                 pack["q"][b.par][0:rows, g * QUAD + h, :], start=True, stop=True)\
                    .then_inc(exp_tile, 1)

            def times_values(b, g, t):
                m = g * NT + t
                pe.wait_ge(exp_ready, b.count(TILES_B, (m + 1) * QUAD))
                if t == 0:
                    need(pe, o_copied, b.count(NQ, g - 1))
                    pe.wait_ge(v_ready, b.count(1, 1))
                for h in range(QUAD):
                    last = nc.tensor.matmul(p_o[g % 2][h * COLS:(h + 1) * COLS, :],
                                            values[b.par][:, t, g * QUAD + h, :],
                                            exps[(m * QUAD + h) % RING][:], start=t == 0, stop=t == NT - 1,
                                            tile_position=(0, h * COLS))
                last.then_inc(pv_done, 1)

            def turn_max(b, g):
                pe.wait_ge(max_read, b.count(TILES_B, (g + 1) * TILES_Q))
                if g == 1 and there(b, 1):
                    pe.wait_ge(xt_copied, b.count(1, 2))
                elif g == 2 and there(b, 1):
                    pe.wait_ge(copied["k"], b.count(1, 2))
                elif g == 3 and there(b, 1):
                    pe.wait_ge(v_ready, b.count(1, 2))
                else:
                    need(pe, max_negated, b.count(NQ, g))
                    if g == 0:
                        pe.wait_ge(v_ready, b.count(1, 1))
                nc.tensor.transpose(p_a[:, 0:P], maxima[g % 2][:], w.ident[:]).then_inc(max_turned, 1)

            def turn_o(b, g):
                pe.wait_ge(o_copied, b.count(NQ, g + 1))
                need(pe, norm_step, b.count(NORM_STEPS * NQ, NORM_STEPS * g))
                if g == 0:
                    need(pe, out_ready, b.count(1))
                for t in range(NT):
                    last = nc.tensor.transpose(p_b[:, t * P:(t + 1) * P], o_raw[g % 2][:, t * P:(t + 1) * P],
                                               w.ident[:])
                last.then_inc(o_turned, 1)

            def turn_norm(b):
                pe.wait_ge(norm_step, b.count(NORM_STEPS * NQ, NORM_STEPS * NQ))
                for t in range(NT):
                    last = nc.tensor.transpose(p_b[:, t * P:(t + 1) * P], o_norm[:, t, :], w.ident[:])
                last.then_inc(norm_turned, 1)

            def project_out(b):
                pe.wait_ge(ot_copied, b.count(1, 1))
                for t in range(NT):
                    last = nc.tensor.matmul(p_b[:, t * P:(t + 1) * P], ot[:, t * P:(t + 1) * P], w.wo[:],
                                            start=True, stop=True)
                last.then_inc(out_projected, 1)

            def maxima_of(b, g, t):
                if g == 0 and t == 0:
                    pe.wait_ge(packed[b.par], b.half(PACK_DMA, PACK_DMA))
                for h in range(QUAD):
                    score_max(b, g, t, h)

            def batch(b, is_first, is_last):
                for g in range(NQ):
                    ahead = quad(b, g + 2)
                    for t in range(NT):
                        if t == 0:
                            pe.wait_ge(max_packed[g % 2], b.count(MAX_DMA * NQ // 2, MAX_DMA * (g // 2 + 1)))
                            if g == 2 and there(ahead[0]):
                                pe.wait_ge(packed[ahead[0].par], ahead[0].half(PACK_DMA, PACK_DMA))
                        for h in range(QUAD):
                            if there(ahead[0]):
                                score_max(*ahead, t, h)
                            score_exp(b, g, t, h)
                        if t > 0:
                            times_values(b, g, t - 1)
                        elif g > 0:
                            times_values(b, g - 1, NT - 1)
                        elif not is_first:
                            times_values(b.step(-1), NQ - 1, NT - 1)
                        pieces(b, g, t, is_first)

            def pieces(b, g, t, is_first):
                if t == (1 if g == 0 else 0) and there(quad(b, g + 1)[0]):
                    turn_max(*quad(b, g + 1))
                if t == 2 and g > 0:
                    turn_o(b, g - 1)
                if not is_first:
                    if (g, t) == (0, 2):
                        turn_o(b.step(-1), NQ - 1)
                    if (g, t) == (0, 3):
                        turn_norm(b.step(-1))
                    if (g, t) == (1, 0):
                        project_out(b.step(-1))
                if there(b, 1):
                    c = b.step(1)
                    if (g, t) == (0, 0):
                        turn_x(c)
                    if (g, t) == (0, 2):
                        project_qk(c, "q", w.wq)
                    if (g, t) == (0, 3):
                        project_qk(c, "k", w.wk)
                    if (g, t) == (1, 1):
                        project_v(c)

            begin, end = Turn(0, 0), Turn(0, NB - 1)
            turn_x(begin)
            project_qk(begin, "q", w.wq)
            project_qk(begin, "k", w.wk)
            project_v(begin)
            for g in range(2):
                for t in range(NT):
                    maxima_of(begin, g, t)
                if g == 0:
                    turn_max(begin, 0)
            all_batches(pe, batch)
            times_values(end, NQ - 1, NT - 1)
            turn_o(end, NQ - 1)
            turn_norm(end)
            project_out(end)

        @block.scalar
        def _(act):
            def x_copy(b):
                act.wait_ge(xn_turned, b.count(1, 1))
                need(act, projected["v"], b.count(1))
                need(act, xt_low_ready, b.count(1))
                nc.scalar.activation(xt[:], p_a[:], ACT.Copy).then_inc(xt_copied, 1)
                act.wait_ge(xt_copied, b.count(1, 1))
                need(act, projected["k"], b.count(1))
                nc.scalar.activation(xt_high[:], xt[:], ACT.Copy).then_inc(xt_high_ready, 1)

            def operand(b, o, bias):
                act.wait_ge(projected[o], b.count(1, 1))
                need(act, third[o], b.count(1))
                nc.scalar.activation(full[o][:], p_a[:], ACT.Identity, bias=bias[:]).then_inc(copied[o], 1)
                act.wait_ge(copied[o], b.count(1, 1))
                need(act, packed[1 - b.par], b.step(-1).half(PACK_DMA, PACK_DMA)
                     if there_before(b) else 0)
                nc.scalar.activation(parts[o][:, 0, :], full[o][:], ACT.Copy).then_inc(first[o], 1)

            def there_before(b):
                return not isinstance(b.j, int) or b.k > 0

            def operand_second(b, o):
                act.wait_ge(rested[o], b.count(1, 1))
                nc.scalar.activation(parts[o][:, 1, :], rest[o][:], ACT.Copy).then_inc(second[o], 1)

            def negate_max(b, g):
                act.wait_ge(max_turned, b.count(NQ, g + 1))
                need(act, max_step, b.count(MAX_STEPS * NQ, MAX_STEPS * g))
                nc.scalar.activation(max_neg[:], p_a[0:TILES_Q, 0:P], ACT.Copy, scale=-1.0).then_inc(max_negated, 1)

            def exponential(b, g, t, h):
                n = g * TILES_Q + t * QUAD + h
                act.wait_ge(exp_tile, b.count(TILES_B, n + 1))
                need(act, pv_done, b.count(TILES_B // QUAD, n // QUAD - 1))
                nc.scalar.activation(exps[n % RING][:], p_exp[n % 2][:], ACT.Exp, scale=inv_sqrt)\
                    .then_inc(exp_ready, 1)

            def copy_o(b, g):
                act.wait_ge(pv_done, b.count(TILES_B // QUAD, (g + 1) * NT))
                need(act, o_turned, b.count(NQ, g - 1))
                nc.scalar.activation(o_raw[g % 2][:], p_o[g % 2][:], ACT.Copy).then_inc(o_copied, 1)

            def copy_ot(b):
                act.wait_ge(norm_turned, b.count(1, 1))
                need(act, out_projected, b.count(1))
                nc.scalar.activation(ot[:], p_b[:], ACT.Copy).then_inc(ot_copied, 1)

            def batch(b, is_first, is_last):
                for g in range(NQ):
                    for t in range(NT):
                        for h in range(QUAD):
                            exponential(b, g, t, h)
                        pieces(b, g, t, is_first)

            def pieces(b, g, t, is_first):
                if t == (1 if g == 0 else 0) and there(quad(b, g + 1)[0]):
                    negate_max(*quad(b, g + 1))
                if t == 1:
                    if g > 0:
                        copy_o(b, g - 1)
                    elif not is_first:
                        copy_o(b.step(-1), NQ - 1)
                if (g, t) == (0, 3) and not is_first:
                    copy_ot(b.step(-1))
                if there(b, 1):
                    c = b.step(1)
                    if (g, t) == (0, 0):
                        x_copy(c)
                    if (g, t) == (0, 2):
                        operand(c, "q", w.bq)
                    if (g, t) == (0, 3):
                        operand_second(c, "q")
                        operand(c, "k", w.bk)
                    if (g, t) == (1, 0):
                        operand_second(c, "k")

            begin, end = Turn(0, 0), Turn(0, NB - 1)
            x_copy(begin)
            for o, bias in (("q", w.bq), ("k", w.bk)):
                operand(begin, o, bias)
                operand_second(begin, o)
            negate_max(begin, 0)
            all_batches(act, batch)
            copy_o(end, NQ - 1)
            copy_ot(end)

        @block.gpsimd
        def _(pool):
            G = nc.gpsimd

            def rstd_batch(b):
                pool.wait_ge(var_ready, b.count(1, 1))
                need(pool, normed, b.count(1))
                G.tensor_tensor(norm.rstd[:], norm.var_eps[:], w.minus_half[:], ALU.pow).then_inc(rstd_ready, 1)

            def x_rest(b):
                pool.wait_ge(xt_high_ready, b.count(1, 1))
                G.tensor_tensor(xt_low[:], xt[:], xt_high[:].bitcast(F32), ALU.subtract).then_inc(xt_low_ready, 1)

            def operand_rest(b, o):
                pool.wait_ge(first[o], b.count(1, 1))
                G.tensor_tensor(rest[o][:], full[o][:], parts[o][:, 0, :], ALU.subtract).then_inc(rested[o], 1)
                pool.wait_ge(second[o], b.count(1, 1))
                G.tensor_tensor(parts[o][:, 2, :], rest[o][:], parts[o][:, 1, :], ALU.subtract).then_inc(third[o], 1)

            def split_max(b, g):
                out = max_parts[g % 2]
                at = lambda n: b.count(MAX_STEPS * NQ, MAX_STEPS * g + n)
                pool.wait_ge(max_negated, b.count(NQ, g + 1))
                need(pool, max_packed[g % 2], b.count(MAX_DMA * NQ // 2, MAX_DMA * (g // 2)))
                G.tensor_tensor(out[:, 0, :], max_neg[:], zeros[:], ALU.add).then_inc(max_step, 1)
                pool.wait_ge(max_step, at(1))
                G.tensor_tensor(max_rest[:], max_neg[:], out[:, 0, :], ALU.subtract).then_inc(max_step, 1)
                pool.wait_ge(max_step, at(2))
                G.tensor_tensor(out[:, 1, :], max_rest[:], zeros[:], ALU.add).then_inc(max_step, 1)
                pool.wait_ge(max_step, at(3))
                G.tensor_tensor(out[:, 2, :], max_rest[:], out[:, 1, :], ALU.subtract).then_inc(max_step, 1)

            def add_bias(b):
                pool.wait_ge(x_res_loaded[b.par], b.half(16, 16))
                need(pool, out_ready, b.count(1))
                G.tensor_tensor(x_bias[:], x_res[b.par][:], w.bo[:].unsqueeze(1).to_broadcast([P, NT, D]),
                                ALU.add).then_inc(bias_ready, 1)

            def batch(b, is_first, is_last):
                c = b.step(1)
                if there(b, 1):
                    x_rest(c)
                split_max(b, 1)
                if there(b, 1):
                    operand_rest(c, "q")
                    operand_rest(c, "k")
                split_max(b, 2)
                add_bias(b)
                split_max(b, 3)
                if there(b, 1):
                    split_max(c, 0)
                if there(b, 2):
                    rstd_batch(b.step(2))

            for par in range(2):
                G.memset(values[par][:], 1.0).then_inc(pool_init, 1)
            G.memset(maxima[0][:], 0.0).then_inc(pool_init, 1)
            G.memset(maxima[1][:], 0.0).then_inc(pool_init, 1)
            G.memset(zeros[:], 0.0).then_inc(pool_init, 1)
            pool.wait_ge(pool_init, 5)
            begin = Turn(0, 0)
            rstd_batch(begin)
            x_rest(begin)
            rstd_batch(begin.step(1))
            operand_rest(begin, "q")
            operand_rest(begin, "k")
            split_max(begin, 0)
            all_batches(pool, batch)

        @block.vector
        def _(dve):
            V = nc.vector

            norm_stats, norm_var, norm_apply = normalisation(
                nc, dve, x_in, xn, norm, x_in_loaded, stats_done, var_ready, rstd_ready, normed, xn_turned)

            def take_max(b, g, t, h):
                n = g * TILES_Q + t * QUAD + h
                dve.wait_ge(max_tile, b.count(TILES_B, n + 1))
                if t == 0 and h == 0:
                    need(dve, max_turned, b.count(NQ, g - 1))
                V.tensor_reduce(maxima[g % 2][:, h * NT + t:h * NT + t + 1], p_max[n % 2][:], AX.X, ALU.max)\
                    .then_inc(max_read, 1)

            def copy_values(b):
                dve.wait_ge(projected["v"], b.count(1, 1))
                need(dve, pv_done, b.count(TILES_B // QUAD, -TILES_B // QUAD))
                V.tensor_tensor(values[b.par][:, :, :, 0:HD],
                                p_a[:].rearrange("p (t h d) -> p t h d", t=NT, d=HD),
                                w.bv[:].rearrange("p (h d) -> p h d", d=HD).unsqueeze(1)
                                .to_broadcast([P, NT, HEADS, HD]), ALU.add).then_inc(v_ready, 1)

            def normalise(b, g):
                at = lambda n: b.count(NORM_STEPS * NQ, NORM_STEPS * g + n)
                quads = p_b[:].rearrange("p (t h c) -> p t h c", t=NT, c=COLS)
                dve.wait_ge(o_turned, b.count(NQ, g + 1))
                V.reciprocal(sums_inv[:], quads[:, :, :, HD]).then_inc(norm_step, 1)
                dve.wait_ge(norm_step, at(1))
                V.tensor_tensor(sums_scale[:], sums_inv[:], w.head_mask[:, g * QUAD:(g + 1) * QUAD]
                                .unsqueeze(1).to_broadcast([P, NT, QUAD]), ALU.mult).then_inc(norm_step, 1)
                dve.wait_ge(norm_step, at(2))
                need(dve, norm_turned, b.count(1))
                out = o_norm[:, :, g * QUAD * HD:(g + 1) * QUAD * HD].rearrange("p t (h d) -> p t h d", d=HD)
                V.tensor_tensor(out, quads[:, :, :, 0:HD], sums_scale[:].unsqueeze(3)
                                .to_broadcast([P, NT, QUAD, HD]), ALU.mult).then_inc(norm_step, 1)

            def residual(b):
                dve.wait_ge(out_projected, b.count(1, 1))
                dve.wait_ge(bias_ready, b.count(1, 1))
                need(dve, stored[b.par], b.half(16))
                V.tensor_tensor(x_out[b.par][:], p_b[:].rearrange("p (t d) -> p t d", d=D), x_bias[:],
                                ALU.add).then_inc(out_ready, 1)

            def batch(b, is_first, is_last):
                for g in range(NQ):
                    ahead = quad(b, g + 2)
                    for t in range(NT):
                        if there(ahead[0]):
                            for h in range(QUAD):
                                take_max(*ahead, t, h)
                        pieces(b, g, t, is_first)

            def pieces(b, g, t, is_first):
                if t == 2 and g > 0:
                    normalise(b, g - 1)
                if not is_first:
                    if (g, t) == (0, 2):
                        normalise(b.step(-1), NQ - 1)
                    if (g, t) == (1, 0):
                        residual(b.step(-1))
                if (g, t) == (1, 1) and there(b, 1):
                    copy_values(b.step(1))
                if g == 3 and there(b, 2):
                    if t == 0:
                        norm_stats(b.step(2))
                    if t == 1:
                        norm_var(b.step(2))
                    if t == 3:
                        norm_apply(b.step(2))

            begin, end = Turn(0, 0), Turn(0, NB - 1)
            one_rows = slice(MAX_ROW, MAX_ROW + PARTS)
            for par in range(2):
                V.memset(pack["q"][par][64:P, :, :].bitcast(F32), 0.0).then_inc(dve_init, 1)
                V.memset(pack["k"][par][64:MAX_ROW, :, :].bitcast(F32), 0.0).then_inc(dve_init, 1)
                V.memset(pack["k"][par][one_rows, :, :], 1.0).then_inc(dve_init, 1)
            for n in range(2):
                norm_stats(begin.step(n))
                norm_var(begin.step(n))
                norm_apply(begin.step(n))
            dve.wait_ge(pool_init, 4)
            copy_values(begin)
            for g in range(2):
                for t in range(NT):
                    for h in range(QUAD):
                        take_max(begin, g, t, h)
            all_batches(dve, batch)
            normalise(end, NQ - 1)
            residual(end)


class Weights:

    def __init__(self, nc, ctx):
        sb = lambda name, shape, dt=F32: ctx.enter_context(nc.sbuf_tensor(name, shape, dt))
        both = lambda name, shape: [sb(f"{name}_high", shape, F32R), sb(f"{name}_low", shape, F32R)]
        self.gate, self.up = both("gate", [P, HID]), both("up", [P, HID])
        self.down = both("down", [P, TILES, D])
        self.wq, self.wk = both("wq", [P, D]), both("wk", [P, D])
        self.wv, self.wo = sb("wv", [P, D]), sb("wo", [P, D])
        self.bq, self.bk, self.bv, self.bo = sb("bq", [P, 1]), sb("bk", [P, 1]), sb("bv", [P, D]), sb("bo", [P, D])
        self.head_mask, self.gate_w = sb("head_mask", [P, HEADS]), sb("gate_w", [P, E])
        self.rank = sb("rank", [P, NT, E])
        self.ident, self.ident16 = sb("ident", [P, P]), sb("ident16", [P, P], BF16)
        self.selector = sb("selector", [P, ROUTED], BF16)
        self.minus_half = sb("minus_half", [P, NT])


def program(nc, dram, out):
    after_ffn = nc.dram_tensor("after_ffn", [NB * S, D], F32, kind="Internal").ap()
    after_attn = nc.dram_tensor("after_attn", [NB * S, D], F32, kind="Internal").ap()
    with ExitStack() as ctx:
        w = Weights(nc, ctx)
        setup(nc, dram, w)
        x = dram["x"].rearrange("b s d -> (b s) d")
        y = out.rearrange("b s d -> (b s) d")
        ffn(nc, "ffn1", w, x, after_ffn)
        attention(nc, w, after_ffn, after_attn)
        ffn(nc, "ffn2", w, after_attn, y)


def kernel(**inputs):
    import numpy as np
    import concourse.bacc as bacc
    from concourse.bass_utils import run_bass_kernel_spmd

    data = {k.replace("L0_attn_", "").replace("L0_ffn_", ""): np.asarray(v) for k, v in inputs.items()}
    arrays = {k: data[k] for k in ("x", "bq", "bk", "bv", "bo", "head_mask", "w_gate", "w_up", "w_down",
                                   "sw_gate", "sw_up", "sw_down")}
    by_d = lambda a: a.reshape(-1, HEADS, HD).swapaxes(1, 2).reshape(a.shape)
    arrays |= {"bq": by_d(data["bq"]), "bk": by_d(data["bk"])}
    arrays |= {"wq_t": by_d(data["Wq"].T), "wk_t": by_d(data["Wk"].T), "wv_t": data["Wv"].T, "wo_t": data["Wo"].T,
               "gate_w_t": data["gate_w"].T}
    arrays["identity"] = np.eye(P, dtype=np.float32)
    arrays["rank"] = np.ascontiguousarray(np.broadcast_to(np.arange(E, 0, -1, dtype=np.float32), (P, NT, E)))
    expert = np.arange(ROUTED) // F
    arrays["selector"] = (np.arange(PARTS * E)[:, None] % E == expert[None, :]).astype(np.float32)
    arrays = {f"in_{k}": np.ascontiguousarray(a) for k, a in arrays.items()}

    nc = bacc.Bacc("TRN2", target_bir_lowering=False, num_devices=1)
    dram = {k[3:]: nc.dram_tensor(k, a.shape, mybir.dt.from_np(a.dtype), kind="ExternalInput").ap()
            for k, a in arrays.items()}
    out = nc.dram_tensor("out", (NB, S, D), F32, kind="ExternalOutput").ap()
    program(nc, dram, out)
    result = run_bass_kernel_spmd(nc, [arrays], core_ids=[0])
    return result.results[0]["out"]
```

```python
import concourse.bass as bass
from concourse import mybir
from contextlib import ExitStack

F32 = mybir.dt.float32
F32R = mybir.dt.float32r
BF16 = mybir.dt.bfloat16
ALU = mybir.AluOpType
ACT = mybir.ActivationFunctionType
AX = mybir.AxisListType

P = 128
D = 128
E, F, FS = 8, 176, 352
ROUTED, HID = E * F, E * F + FS
TILES = -(-HID // P)
RTILES = ROUTED // P
S = 512
NT = S // P
NB = 16
HEAD = 4
PARTS = 3
HEADS, HD = 16, 8
QUAD = 4
NQ = HEADS // QUAD
TILES_Q = QUAD * NT
COLS = 32
MAX_ROW = 96
EPS = 1e-5
TOPK_EPS = 1e-20
SCALE = 2.5
assert ROUTED % P == 0


def width(f):
    return min(P, HID - f * P)


class Turn:

    def __init__(self, j, k):
        self.j, self.k, self.par = j, k, k % 2

    def count(self, per, more=0):
        const = self.k * per + more
        return const if isinstance(self.j, int) else self.j * (2 * per) + const

    def half(self, per, more=0):
        const = (self.k // 2) * per + more
        return const if isinstance(self.j, int) else self.j * per + const

    def step(self, n):
        return Turn(self.j, self.k + n)

    def of(self, dram):
        return dram[self.k] if isinstance(self.j, int) else dram[self.j * 2 + self.k]


def need(eng, sem, value):
    if isinstance(value, int) and value <= 0:
        return
    eng.wait_ge(sem, value)


def all_batches(eng, batch):
    for k in range(HEAD):
        batch(Turn(0, k), k == 0, False)
    with eng.Fori(0, (NB - HEAD - 2) // 2) as j:
        for k in (HEAD, HEAD + 1):
            batch(Turn(j, k), False, False)
    batch(Turn(0, NB - 2), False, False)
    batch(Turn(0, NB - 1), False, True)


def setup(nc, dram, w):
    with ExitStack() as ctx:
        sb = lambda name, shape: ctx.enter_context(nc.sbuf_tensor(name, shape, F32))
        sem = lambda name: ctx.enter_context(nc.semaphore(name))
        gate, up = sb("gate_full", [P, HID]), sb("up_full", [P, HID])
        down = sb("down_full", [P, TILES, D])
        wq, wk = sb("wq_full", [P, D]), sb("wk_full", [P, D])
        selector = sb("selector_full", [PARTS * E, ROUTED])
        gate_loaded, up_loaded, down_loaded = sem("gate_loaded"), sem("up_loaded"), sem("down_loaded")
        qk_loaded, attn_loaded, consts_loaded = sem("qk_loaded"), sem("attn_loaded"), sem("consts_loaded")
        selector_cleared, high_done, low_done = sem("selector_cleared"), sem("high_done"), sem("low_done")
        zeros_ready, pool_filled = sem("zeros_ready"), sem("pool_filled")
        block = ctx.enter_context(nc.Block())
        full_rows = HID // P * P
        last = width(TILES - 1)

        def zero_rows(pack):
            return pack[64:MAX_ROW, :, :].bitcast(F32)

        splits = [(gate_loaded, 32, gate[:], w.gate[0][:], w.gate[1][:]),
                  (up_loaded, 32, up[:], w.up[0][:], w.up[1][:]),
                  (down_loaded, 48, down[:, 0:TILES - 1, :], w.down[0][:, 0:TILES - 1, :], w.down[1][:, 0:TILES - 1, :]),
                  (down_loaded, 48, down[0:last, TILES - 1, :], w.down[0][0:last, TILES - 1, :],
                   w.down[1][0:last, TILES - 1, :]),
                  (qk_loaded, 32, wq[:], w.wq[0][:], w.wq[1][:]),
                  (qk_loaded, 32, wk[:], w.wk[0][:], w.wk[1][:])]

        @block.sync
        def _(sp):
            for dst, routed, shared, loaded in ((gate, dram["w_gate"], dram["sw_gate"], gate_loaded),
                                                (up, dram["w_up"], dram["sw_up"], up_loaded)):
                sp.dma_start(dst[:, 0:ROUTED].rearrange("d (e f) -> d e f", e=E),
                             routed.rearrange("e d f -> d e f")).then_inc(loaded, 16)
                sp.dma_start(dst[:, ROUTED:HID], shared).then_inc(loaded, 16)
            sp.dma_start(wq[:], dram["wq_t"]).then_inc(qk_loaded, 16)
            sp.dma_start(wk[:], dram["wk_t"]).then_inc(qk_loaded, 16)
            sp.dma_start(w.gate_w[:], dram["gate_w_t"]).then_inc(attn_loaded, 16)
            sp.dma_start(w.rank[:], dram["rank"]).then_inc(attn_loaded, 16)
            sp.dma_start(w.wv[:], dram["wv_t"]).then_inc(attn_loaded, 16)
            sp.dma_start(w.wo[:], dram["wo_t"]).then_inc(attn_loaded, 16)
            sp.dma_start(w.bq[:], dram["bq"].rearrange("(p a) -> p a", a=1)).then_inc(attn_loaded, 16)
            sp.dma_start(w.bk[:], dram["bk"].rearrange("(p a) -> p a", a=1)).then_inc(attn_loaded, 16)
            for dst, name in ((w.bv, "bv"), (w.bo, "bo"), (w.head_mask, "head_mask")):
                sp.dma_start(dst[:], dram[name].rearrange("(a n) -> a n", a=1)
                             .to_broadcast([P, dram[name].shape[0]])).then_inc(attn_loaded, 16)
            sp.wait_ge(attn_loaded, 16 * 9)

        @block.scalar
        def _(act):
            act.dma_start(down[:, 0:RTILES, :],
                          dram["w_down"].rearrange("e f d -> (e f) d").rearrange("(t p) d -> p t d", p=P)
                          ).then_inc(down_loaded, 16)
            act.dma_start(down[:, RTILES:TILES - 1, :],
                          dram["sw_down"][0:full_rows - ROUTED, :].rearrange("(t p) d -> p t d", p=P)
                          ).then_inc(down_loaded, 16)
            act.dma_start(down[0:last, TILES - 1, :], dram["sw_down"][full_rows - ROUTED:FS, :]
                          ).then_inc(down_loaded, 16)
            act.dma_start(w.ident[:], dram["identity"]).then_inc(consts_loaded, 16)
            act.dma_start(selector[:], dram["selector"]).then_inc(consts_loaded, 16)
            for loaded, value, full, high, _ in splits:
                act.wait_ge(loaded, value)
                nc.scalar.activation(high, full, ACT.Copy).then_inc(high_done, 1)
            act.wait_ge(zeros_ready, 1)
            for pack in (w.pack["q"][1], w.pack["k"][1]):
                nc.scalar.activation(zero_rows(pack), zero_rows(w.pack["q"][0]), ACT.Copy)

        @block.gpsimd
        def _(pool):
            two_ones = (0x3F803F80 - 0x3F800000) * 2.0 ** -23 + 1.0
            starts = [(w.values[0][:], 1.0), (w.values[1][:], 1.0), (w.maxima[0][:], 0.0), (w.maxima[1][:], 0.0),
                      (w.zeros[:], 0.0), (zero_rows(w.pack["k"][0]), 0.0)]
            starts += [(k[MAX_ROW:MAX_ROW + PARTS, :, :].bitcast(F32), two_ones) for k in w.pack["k"]]
            for n, (buffer, value) in enumerate(starts):
                nc.gpsimd.memset(buffer, value).then_inc(pool_filled, 1)
                pool.wait_ge(pool_filled, n + 1)

        @block.vector
        def _(dve):
            nc.vector.memset(zero_rows(w.pack["q"][0]), 0.0).then_inc(zeros_ready, 1)
            nc.vector.memset(w.minus_half[:], -0.5)
            nc.vector.memset(w.selector[:], 0.0).then_inc(selector_cleared, 1)
            for n, (_, _, full, high, low) in enumerate(splits):
                dve.wait_ge(high_done, n + 1)
                nc.vector.tensor_tensor(low, full, high.bitcast(F32), ALU.subtract).then_inc(low_done, 1)
                if n == 0:
                    dve.wait_ge(consts_loaded, 32)
                    nc.vector.tensor_copy(w.ident16[:], w.ident[:])
                    dve.wait_ge(selector_cleared, 1)
                    nc.vector.tensor_copy(w.selector[0:PARTS * E, :], selector[:])
            dve.wait_ge(low_done, len(splits))


class NormBuffers:

    def __init__(self, sb):
        self.stats = sb("stats", [P, NT, 6])
        self.mean_sum, self.mean_diff, self.m2 = sb("mean_sum", [P, NT]), sb("mean_diff", [P, NT]), sb("m2", [P, NT])
        self.mean, self.diff2, self.var_within = sb("mean", [P, NT]), sb("diff2", [P, NT]), sb("var_within", [P, NT])
        self.var_eps, self.rstd = sb("var_eps", [P, NT]), sb("rstd", [P, NT])


def normalisation(nc, dve, x_in, xn, n, x_in_loaded, stats_done, var_ready, rstd_ready, normed, xn_turned):
    V = nc.vector
    STEPS = 3

    def norm_stats(b):
        dve.wait_ge(x_in_loaded[b.par], b.half(16, 16))
        for t in range(NT):
            last = V.bn_stats(n.stats[:, t, :], x_in[b.par][:, t, :])
        last.then_inc(stats_done, 1)

    def norm_var(b):
        even_mean, even_m2, odd_mean, odd_m2 = (n.stats[:, :, i] for i in (1, 2, 4, 5))
        dve.wait_ge(stats_done, b.count(STEPS, 1))
        V.tensor_tensor(n.mean_sum[:], even_mean, odd_mean, ALU.add)
        V.tensor_tensor(n.mean_diff[:], even_mean, odd_mean, ALU.subtract)
        V.tensor_tensor(n.m2[:], even_m2, odd_m2, ALU.add).then_inc(stats_done, 1)
        dve.wait_ge(stats_done, b.count(STEPS, 2))
        V.tensor_scalar(n.mean[:], n.mean_sum[:], 0.5, None, ALU.mult)
        V.scalar_tensor_tensor(n.diff2[:], n.mean_diff[:], 0.25, n.mean_diff[:], ALU.mult, ALU.mult)
        V.tensor_scalar(n.var_within[:], n.m2[:], 1.0 / D, EPS, ALU.mult, ALU.add).then_inc(stats_done, 1)
        dve.wait_ge(stats_done, b.count(STEPS, 3))
        need(dve, rstd_ready, b.count(1))
        V.tensor_tensor(n.var_eps[:], n.diff2[:], n.var_within[:], ALU.add).then_inc(var_ready, 1)

    def norm_apply(b):
        dve.wait_ge(rstd_ready, b.count(1, 1))
        need(dve, xn_turned, b.count(1))
        for t in range(NT):
            last = V.tensor_scalar(xn[:, t, :], x_in[b.par][:, t, :], n.mean[:, t:t + 1],
                                   n.rstd[:, t:t + 1], ALU.subtract, ALU.mult)
        last.then_inc(normed, 1)

    return norm_stats, norm_var, norm_apply


def ffn(nc, name, w, src, dst):
    LAG = 3
    RING = 4
    with ExitStack() as ctx:
        sb = lambda n, shape, dt=F32: ctx.enter_context(nc.sbuf_tensor(f"{name}_{n}", shape, dt))
        pb = lambda n, shape=(P, S): ctx.enter_context(nc.psum_tensor(f"{name}_{n}", list(shape), F32))
        sem = lambda n: ctx.enter_context(nc.semaphore(f"{name}_{n}"))
        pair = lambda make, n, *a: [make(f"{n}{i}", *a) for i in range(2)]

        x_in = pair(sb, "x_in", [P, NT, D])
        x_res = pair(sb, "x_res", [P, NT, D])
        x_out = pair(sb, "x_out", [P, NT, D])
        xn = sb("xn", [P, NT, D])
        xt = sb("xt", [P, S])
        xt_high, xt_low = pair(sb, "xt_high", [P, S], F32R), pair(sb, "xt_low", [P, S], F32R)
        norm = NormBuffers(sb)
        small = {n: sb(n, [P, NT, E]) for n in
                 ("z", "tanh", "first_ranks", "first", "z2", "is_second", "second_ranks", "second",
                  "chosen", "denominator", "exps", "inverse", "scores", "picked", "combine", "rest")}
        one = {n: sb(n, [P, NT]) for n in
               ("top", "first_rank", "top2", "second_rank", "total", "total_inv", "sum2", "sum2_eps", "sum2_inv")}
        combine_parts = sb("combine_parts", [P, NT, PARTS * E], BF16)
        combine_t = pair(sb, "combine_t", [P, S], BF16)
        silu = pair(sb, "silu", [P, S])
        gated = pair(sb, "gated", [P, S])
        hidden = [sb(f"hidden{i}", [P, S]) for i in range(RING)]
        hid_high = [sb(f"hid_high{i}", [P, S], F32R) for i in range(RING)]
        hid_low = [sb(f"hid_low{i}", [P, S], F32R) for i in range(RING)]
        yt = sb("yt", [P, S])
        p_gate, p_up = pair(pb, "p_gate"), pair(pb, "p_up")
        p_spread = pb("p_spread")
        p_y = pair(pb, "p_y")
        p_prep = pb("p_prep")

        x_in_loaded, x_res_loaded, stored = pair(sem, "x_in_loaded"), pair(sem, "x_res_loaded"), pair(sem, "stored")
        zeroed = sem("zeroed")
        stats_done, var_ready, rstd_ready = sem("stats_done"), sem("var_ready"), sem("rstd_ready")
        normed, xn_turned, xt_copied = sem("normed"), sem("xn_turned"), sem("xt_copied")
        xt_high_ready, xt_low_ready = sem("xt_high_ready"), sem("xt_low_ready")
        logits_ready, z_ready, tanh_ready = sem("logits_ready"), sem("z_ready"), sem("tanh_ready")
        route_step = sem("route_step")
        combine_turned, combine_copied = sem("combine_turned"), sem("combine_copied")
        gate_ready, up_ready, spread_ready = sem("gate_ready"), sem("up_ready"), sem("spread_ready")
        silu_ready, gated_ready, weighted_ready = sem("silu_ready"), sem("gated_ready"), sem("weighted_ready")
        high_ready, low_ready, down_done = sem("high_ready"), sem("low_ready"), sem("down_done")
        y_copied, y_turned, out_ready = sem("y_copied"), sem("y_turned"), sem("out_ready")
        ROUTE_PARTS = (2, 3, 3, 3, 4, 3, 4, 4)
        ROUTE_STEPS = sum(ROUTE_PARTS)

        src_b = src.rearrange("(b p t) d -> b p t d", p=P, t=NT)
        dst_b = dst.rearrange("(b p t) d -> b p t d", p=P, t=NT)
        slot = lambda turn, f: (turn.par * TILES + f) % RING
        assert 2 * TILES % RING == 0

        block = ctx.enter_context(nc.Block())

        @block.sync
        def _(sp):
            def load_in(b):
                need(sp, normed, b.count(1, -1))
                sp.dma_start(x_in[b.par][:], b.of(src_b)).then_inc(x_in_loaded[b.par], 16)

            def batch(b, first, last):
                if not last:
                    load_in(b.step(1))
                need(sp, out_ready, b.count(1, -1))
                sp.dma_start(x_res[b.par][:], b.of(src_b)).then_inc(x_res_loaded[b.par], 16)
                if not first:
                    store(b.step(-1))

            def store(b):
                sp.wait_ge(out_ready, b.count(1, 1))
                sp.dma_start(b.of(dst_b), x_out[b.par][:]).then_inc(stored[b.par], 16)

            load_in(Turn(0, 0))
            all_batches(sp, batch)
            store(Turn(0, NB - 1))
            for par in range(2):
                sp.wait_ge(stored[par], 16 * NB // 2)

        @block.tensor
        def _(pe):
            def three(out, weights, high, low, start, stop):
                nc.tensor.matmul(out, weights[0], high, start=start, stop=False)
                nc.tensor.matmul(out, weights[1], high, start=False, stop=False)
                return nc.tensor.matmul(out, weights[0], low, start=False, stop=stop)

            def prep_transpose(b):
                pe.wait_ge(normed, b.count(1, 1))
                need(pe, combine_copied, b.count(1))
                for t in range(NT):
                    last = nc.tensor.transpose(p_prep[:, t * P:(t + 1) * P], xn[:, t, :], w.ident[:])
                last.then_inc(xn_turned, 1)

            def prep_logits(b):
                pe.wait_ge(xt_copied, b.count(1, 1))
                for t in range(NT):
                    last = nc.tensor.matmul(p_prep[:, t * E:(t + 1) * E], xt[:, t * P:(t + 1) * P],
                                            w.gate_w[:], start=True, stop=True)
                last.then_inc(logits_ready, 1)

            def prep_combine(b):
                pe.wait_ge(route_step, b.count(ROUTE_STEPS, ROUTE_STEPS))
                out = p_prep[:].bitcast(BF16)
                for t in range(NT):
                    last = nc.tensor.transpose(out[0:PARTS * E, t * P:(t + 1) * P],
                                               combine_parts[:, t, :], w.ident16[:])
                last.then_inc(combine_turned, 1)

            def gate_up(b, f):
                n, cols = width(f), slice(f * P, f * P + width(f))
                need(pe, silu_ready, b.count(TILES, f - 1))
                three(p_gate[f % 2][0:n, :], [g[:, cols] for g in w.gate], xt_high[b.par][:], xt_low[b.par][:],
                      True, True).then_inc(gate_ready, 1)
                need(pe, gated_ready, b.count(TILES, f - 1))
                three(p_up[f % 2][0:n, :], [u[:, cols] for u in w.up], xt_high[b.par][:], xt_low[b.par][:],
                      True, True).then_inc(up_ready, 1)

            def spread(b, f):
                need(pe, weighted_ready, b.count(RTILES, f))
                if f == 0:
                    pe.wait_ge(combine_copied, b.count(1, 1))
                nc.tensor.matmul(p_spread[:], w.selector[:, f * P:(f + 1) * P], combine_t[b.par][:],
                                 start=True, stop=True).then_inc(spread_ready, 1)

            def down(b, f):
                n, s = width(f), slot(b, f)
                pe.wait_ge(low_ready, b.count(TILES, f + 1))
                if f == 0:
                    need(pe, out_ready, b.count(1, -1))
                three(p_y[b.par][:], [d[0:n, f, :] for d in w.down], hid_high[s][0:n, :], hid_low[s][0:n, :],
                      f == 0, f == TILES - 1).then_inc(down_done, 1)

            def final_transpose(b):
                pe.wait_ge(y_copied, b.count(1, 1))
                for t in range(NT):
                    last = nc.tensor.transpose(p_y[b.par][:, t * P:(t + 1) * P], yt[:, t * P:(t + 1) * P], w.ident[:])
                last.then_inc(y_turned, 1)

            def batch(b, first, last):
                pe.wait_ge(xt_low_ready, b.count(1, 1))
                for f in range(TILES):
                    gate_up(b, f)
                    if f == 0 and first:
                        prep_combine(b)
                    if f >= LAG:
                        down(b, f - LAG)
                    elif not first:
                        down(b.step(-1), TILES + f - LAG)
                    if f < RTILES:
                        spread(b, f)
                    if f == 4 and not first:
                        final_transpose(b.step(-1))
                    if not last:
                        if f == 3:
                            prep_transpose(b.step(1))
                        if f == 4:
                            prep_logits(b.step(1))
                        if f == TILES - 1:
                            prep_combine(b.step(1))

            pe.wait_ge(zeroed, 2)
            prep_transpose(Turn(0, 0))
            prep_logits(Turn(0, 0))
            all_batches(pe, batch)
            end = Turn(0, NB - 1)
            for f in range(TILES - LAG, TILES):
                down(end, f)
            final_transpose(end)

        @block.scalar
        def _(act):
            def xt_copy(b):
                act.wait_ge(xn_turned, b.count(1, 1))
                need(act, logits_ready, b.count(1))
                need(act, xt_low_ready, b.count(1))
                nc.scalar.activation(xt[:], p_prep[:], ACT.Copy).then_inc(xt_copied, 1)

            def xt_split(b):
                act.wait_ge(xt_copied, b.count(1, 1))
                need(act, up_ready, b.count(TILES, -TILES))
                nc.scalar.activation(xt_high[b.par][:], xt[:], ACT.Copy).then_inc(xt_high_ready, 1)

            def tanh(b):
                act.wait_ge(z_ready, b.count(1, 1))
                nc.scalar.activation(small["tanh"][:], small["z"][:], ACT.Tanh, scale=0.5).then_inc(tanh_ready, 1)

            def combine_copy(b):
                act.wait_ge(combine_turned, b.count(1, 1))
                need(act, spread_ready, b.count(RTILES, -RTILES))
                nc.scalar.activation(combine_t[b.par][0:PARTS * E, :], p_prep[:].bitcast(BF16)[0:PARTS * E, 0:S],
                                     ACT.Copy).then_inc(combine_copied, 1)

            def silu_tile(b, f):
                n = width(f)
                act.wait_ge(gate_ready, b.count(TILES, f + 1))
                need(act, gated_ready, b.count(TILES, f - 1))
                nc.scalar.activation(silu[f % 2][0:n, :], p_gate[f % 2][0:n, :], ACT.Silu).then_inc(silu_ready, 1)

            def high_tile(b, f):
                n, s = width(f), slot(b, f)
                if f < RTILES:
                    act.wait_ge(weighted_ready, b.count(RTILES, f + 1))
                else:
                    act.wait_ge(gated_ready, b.count(TILES, f + 1))
                need(act, down_done, b.count(TILES, f + 1 - RING))
                nc.scalar.activation(hid_high[s][0:n, :], hidden[s][0:n, :], ACT.Copy).then_inc(high_ready, 1)

            def y_copy(b):
                act.wait_ge(down_done, b.count(TILES, TILES))
                need(act, y_turned, b.count(1))
                nc.scalar.activation(yt[:], p_y[b.par][:], ACT.Copy).then_inc(y_copied, 1)

            def batch(b, first, last):
                for f in range(TILES):
                    silu_tile(b, f)
                    if f == 0:
                        combine_copy(b)
                    if f > 0:
                        high_tile(b, f - 1)
                    elif not first:
                        high_tile(b.step(-1), TILES - 1)
                    if f == 3 and not first:
                        y_copy(b.step(-1))
                    if not last:
                        if f == 3:
                            xt_copy(b.step(1))
                        if f == 4:
                            xt_split(b.step(1))
                        if f == 6:
                            tanh(b.step(1))

            xt_copy(Turn(0, 0))
            xt_split(Turn(0, 0))
            tanh(Turn(0, 0))
            all_batches(act, batch)
            high_tile(Turn(0, NB - 1), TILES - 1)
            y_copy(Turn(0, NB - 1))

        @block.gpsimd
        def _(pool):
            def rstd_batch(b):
                pool.wait_ge(var_ready, b.count(1, 1))
                need(pool, normed, b.count(1))
                nc.gpsimd.tensor_tensor(norm.rstd[:], norm.var_eps[:], w.minus_half[:], ALU.pow).then_inc(rstd_ready, 1)

            def xt_rest(b):
                pool.wait_ge(xt_high_ready, b.count(1, 1))
                nc.gpsimd.tensor_tensor(xt_low[b.par][:], xt[:], xt_high[b.par][:].bitcast(F32),
                                        ALU.subtract).then_inc(xt_low_ready, 1)

            def low_tile(b, f):
                n, s = width(f), slot(b, f)
                pool.wait_ge(high_ready, b.count(TILES, f + 1))
                nc.gpsimd.tensor_tensor(hid_low[s][0:n, :], hidden[s][0:n, :],
                                        hid_high[s][0:n, :].bitcast(F32), ALU.subtract).then_inc(low_ready, 1)

            def batch(b, first, last):
                for f in range(TILES):
                    if f > 0:
                        low_tile(b, f - 1)
                    elif not first:
                        low_tile(b.step(-1), TILES - 1)
                    if not last:
                        if f == 1:
                            rstd_batch(b.step(1))
                        if f == 5:
                            xt_rest(b.step(1))

            for par in range(2):
                nc.gpsimd.memset(combine_t[par][:], 0.0).then_inc(zeroed, 1)
            rstd_batch(Turn(0, 0))
            xt_rest(Turn(0, 0))
            all_batches(pool, batch)
            low_tile(Turn(0, NB - 1), TILES - 1)

        @block.vector
        def _(dve):
            V = nc.vector
            per_token = lambda a: a[:].unsqueeze(2).to_broadcast([P, NT, E])
            logits = p_prep[:, 0:NT * E].rearrange("p (t e) -> p t e", e=E)

            norm_stats, norm_var, norm_apply = normalisation(
                nc, dve, x_in, xn, norm, x_in_loaded, stats_done, var_ready, rstd_ready, normed, xn_turned)

            def route(b, part):
                z, rank = small["z"], w.rank
                done = [sum(ROUTE_PARTS[:part])]

                def step(instruction):
                    instruction.then_inc(route_step, 1)
                    done[0] += 1
                    dve.wait_ge(route_step, b.count(ROUTE_STEPS, done[0]))

                if part == 0:
                    dve.wait_ge(logits_ready, b.count(1, 1))
                    need(dve, tanh_ready, b.count(1))
                    step(V.tensor_reduce(one["top"][:], logits, AX.X, ALU.max))
                    V.tensor_tensor(z[:], logits, per_token(one["top"]), ALU.subtract).then_inc(z_ready, 1)
                    dve.wait_ge(z_ready, b.count(1, 1))
                    step(V.scalar_tensor_tensor(small["first_ranks"][:], z[:], 0.0, rank[:], ALU.is_equal, ALU.mult))
                if part == 1:
                    step(V.tensor_reduce(one["first_rank"][:], small["first_ranks"][:], AX.X, ALU.max))
                    step(V.tensor_tensor(small["first"][:], rank[:], per_token(one["first_rank"]), ALU.is_equal))
                    step(V.scalar_tensor_tensor(small["z2"][:], small["first"][:], -3e38, z[:], ALU.mult, ALU.add))
                if part == 2:
                    step(V.tensor_reduce(one["top2"][:], small["z2"][:], AX.X, ALU.max))
                    step(V.tensor_tensor(small["is_second"][:], small["z2"][:], per_token(one["top2"]), ALU.is_equal))
                    step(V.tensor_tensor(small["second_ranks"][:], small["is_second"][:], rank[:], ALU.mult))
                if part == 3:
                    step(V.tensor_reduce(one["second_rank"][:], small["second_ranks"][:], AX.X, ALU.max))
                    step(V.tensor_tensor(small["second"][:], rank[:], per_token(one["second_rank"]), ALU.is_equal))
                    step(V.tensor_tensor(small["chosen"][:], small["first"][:], small["second"][:], ALU.add))
                if part == 4:
                    dve.wait_ge(tanh_ready, b.count(1, 1))
                    step(V.tensor_scalar(small["denominator"][:], small["tanh"][:], -1.0, 1.0, ALU.mult, ALU.add))
                    step(V.reciprocal(small["inverse"][:], small["denominator"][:]))
                    step(V.scalar_tensor_tensor(small["exps"][:], small["tanh"][:], 1.0, small["inverse"][:],
                                                ALU.add, ALU.mult))
                    step(V.tensor_reduce(one["total"][:], small["exps"][:], AX.X, ALU.add))
                if part == 5:
                    step(V.reciprocal(one["total_inv"][:], one["total"][:]))
                    step(V.tensor_tensor(small["scores"][:], small["exps"][:], per_token(one["total_inv"]), ALU.mult))
                    step(V.tensor_tensor(small["picked"][:], small["scores"][:], small["chosen"][:], ALU.mult))
                parts = [combine_parts[:, :, i * E:(i + 1) * E] for i in range(PARTS)]
                cw, rest = small["combine"], small["rest"]
                if part == 6:
                    step(V.tensor_reduce(one["sum2"][:], small["picked"][:], AX.X, ALU.add))
                    step(V.tensor_scalar(one["sum2_eps"][:], one["sum2"][:], TOPK_EPS, None, ALU.add))
                    step(V.reciprocal(one["sum2_inv"][:], one["sum2_eps"][:]))
                    step(V.scalar_tensor_tensor(cw[:], small["picked"][:], SCALE, per_token(one["sum2_inv"]),
                                                ALU.mult, ALU.mult))
                if part == 7:
                    need(dve, combine_turned, b.count(1))
                    step(V.tensor_copy(parts[0], cw[:]))
                    step(V.tensor_tensor(rest[:], cw[:], parts[0], ALU.subtract))
                    step(V.tensor_copy(parts[1], rest[:]))
                    step(V.tensor_tensor(parts[2], rest[:], parts[1], ALU.subtract))

            def gated_tile(b, f):
                n, s = width(f), slot(b, f)
                dve.wait_ge(silu_ready, b.count(TILES, f + 1))
                dve.wait_ge(up_ready, b.count(TILES, f + 1))
                if f < RTILES:
                    out = gated[f % 2]
                else:
                    need(dve, low_ready, b.count(TILES, f + 1 - RING))
                    out = hidden[s]
                V.tensor_tensor(out[0:n, :], silu[f % 2][0:n, :], p_up[f % 2][0:n, :], ALU.mult).then_inc(gated_ready, 1)

            def weighted_tile(b, f):
                dve.wait_ge(gated_ready, b.count(TILES, f + 1))
                dve.wait_ge(spread_ready, b.count(RTILES, f + 1))
                need(dve, low_ready, b.count(TILES, f + 1 - RING))
                V.tensor_tensor(hidden[slot(b, f)][:], gated[f % 2][:], p_spread[:], ALU.mult).then_inc(weighted_ready, 1)

            def residual(b):
                dve.wait_ge(y_turned, b.count(1, 1))
                dve.wait_ge(x_res_loaded[b.par], b.half(16, 16))
                need(dve, stored[b.par], b.half(16))
                V.scalar_tensor_tensor(x_out[b.par][:], p_y[b.par][:].rearrange("p (t d) -> p t d", d=D), 0.5,
                                       x_res[b.par][:], ALU.mult, ALU.add).then_inc(out_ready, 1)

            def batch(b, first, last):
                for f in range(TILES):
                    if 0 < f <= RTILES:
                        weighted_tile(b, f - 1)
                    gated_tile(b, f)
                    if f == 5 and not first:
                        residual(b.step(-1))
                    if not last:
                        if f == 0:
                            norm_stats(b.step(1))
                        if f == 1:
                            norm_var(b.step(1))
                        if f == 2:
                            norm_apply(b.step(1))
                        if 5 <= f < 5 + len(ROUTE_PARTS):
                            route(b.step(1), f - 5)

            begin = Turn(0, 0)
            norm_stats(begin)
            norm_var(begin)
            norm_apply(begin)
            for part in range(len(ROUTE_PARTS)):
                route(begin, part)
            all_batches(dve, batch)
            residual(Turn(0, NB - 1))


def attention(nc, w, src, dst):
    TILES_B = NQ * TILES_Q
    RING = 2 * QUAD
    PACK_DMA, MAX_DMA = 2 * PARTS * PARTS * 16, PARTS * 16
    inv_sqrt = 1.0 / HD ** 0.5
    with ExitStack() as ctx:
        sb = lambda n, shape, dt=F32: ctx.enter_context(nc.sbuf_tensor(f"attn_{n}", shape, dt))
        pb = lambda n: ctx.enter_context(nc.psum_tensor(f"attn_{n}", [P, S], F32))
        sem = lambda n: ctx.enter_context(nc.semaphore(f"attn_{n}"))
        pair = lambda make, n, *a: [make(f"{n}{i}", *a) for i in range(2)]

        x_in = pair(sb, "x_in", [P, NT, D])
        x_res = pair(sb, "x_res", [P, NT, D])
        x_bias = sb("x_bias", [P, NT, D])
        x_out = pair(sb, "x_out", [P, NT, D])
        xn = sb("xn", [P, NT, D])
        xt, xt_high, xt_low = sb("xt", [P, S]), sb("xt_high", [P, S], F32R), sb("xt_low", [P, S], F32R)
        norm = NormBuffers(sb)
        full = {o: sb(f"{o}_full", [P, S]) for o in "qk"}
        rest = {o: sb(f"{o}_rest", [P, S]) for o in "qk"}
        parts = {o: sb(f"{o}_parts", [P, PARTS, S], BF16) for o in "qk"}
        pack, values, maxima, zeros = w.pack, w.values, w.maxima, w.zeros
        max_neg, max_rest = sb("max_neg", [TILES_Q, P]), sb("max_rest", [TILES_Q, P])
        max_parts = pair(sb, "max_parts", [TILES_Q, PARTS, P], BF16)
        exps = [sb(f"exps{i}", [P, S]) for i in range(RING)]
        o_raw = pair(sb, "o_raw", [P, S])
        sums_inv, sums_scale = sb("sums_inv", [P, NT, QUAD]), sb("sums_scale", [P, NT, QUAD])
        o_norm = sb("o_norm", [P, NT, D])
        ot = sb("ot", [P, S])
        p_max, p_exp = [pb(f"p_max{i}") for i in range(4)], [pb(f"p_exp{i}") for i in range(2)]
        p_o = pb("p_o")
        p_x = pb("p_x")

        x_in_loaded, x_res_loaded, stored = pair(sem, "x_in_loaded"), pair(sem, "x_res_loaded"), pair(sem, "stored")
        stats_done, var_ready, rstd_ready = sem("stats_done"), sem("var_ready"), sem("rstd_ready")
        normed, xn_turned, xt_copied = sem("normed"), sem("xn_turned"), sem("xt_copied")
        xt_high_ready, xt_low_ready = sem("xt_high_ready"), sem("xt_low_ready")
        projected = {o: sem(f"{o}_projected") for o in "qkv"}
        copied = {o: sem(f"{o}_copied") for o in "qk"}
        first, second, third = ({o: sem(f"{o}_{n}") for o in "qk"} for n in ("first", "second", "third"))
        rested = {o: sem(f"{o}_rested") for o in "qk"}
        v_ready = sem("v_ready")
        packed = pair(sem, "packed")
        max_tile, max_read = sem("max_tile"), sem("max_read")
        max_turned, max_negated, max_step = sem("max_turned"), sem("max_negated"), sem("max_step")
        max_packed = pair(sem, "max_packed")
        exp_tile, exp_ready, pv_done = sem("exp_tile"), sem("exp_ready"), sem("pv_done")
        o_copied, o_turned, norm_step = sem("o_copied"), sem("o_turned"), sem("norm_step")
        norm_turned, ot_copied, out_projected = sem("norm_turned"), sem("ot_copied"), sem("out_projected")
        bias_ready, out_ready = sem("bias_ready"), sem("out_ready")
        NORM_STEPS, MAX_STEPS = 3, 4

        src_b = src.rearrange("(b p t) d -> b p t d", p=P, t=NT)
        dst_b = dst.rearrange("(b p t) d -> b p t d", p=P, t=NT)

        def there(b, n=0):
            return not isinstance(b.j, int) or b.k + n < NB

        def quad(b, g):
            return b.step(g // NQ), g % NQ

        def pack_operand(eng, b, o, n):
            eng.wait_ge((first, second, third)[n][o], b.count(1, 1))
            for m in range(PARTS):
                r = (n * PARTS + m if o == "q" else m * PARTS + n) * HD
                eng.dma_start(pack[o][b.par][r:r + HD, :, :], parts[o][:, n, :]).then_inc(packed[b.par], 16)

        block = ctx.enter_context(nc.Block())

        @block.sync
        def _(sp):
            def load_in(b):
                need(sp, normed, b.count(1, -1))
                sp.dma_start(x_in[b.par][:], b.of(src_b)).then_inc(x_in_loaded[b.par], 16)

            def load_res(b):
                need(sp, bias_ready, b.count(1, -1))
                sp.dma_start(x_res[b.par][:], b.of(src_b)).then_inc(x_res_loaded[b.par], 16)

            def store(b):
                sp.wait_ge(out_ready, b.count(1, 1))
                sp.dma_start(b.of(dst_b), x_out[b.par][:]).then_inc(stored[b.par], 16)

            def pack_max(b, g):
                sp.wait_ge(max_step, b.count(MAX_STEPS * NQ, MAX_STEPS * (g + 1)))
                for i in range(PARTS):
                    sp.dma_start(pack["q"][b.par][MAX_ROW + i:MAX_ROW + i + 1, g * QUAD:(g + 1) * QUAD, :],
                                 max_parts[g % 2][:, i, :]).then_inc(max_packed[g % 2], 16)

            def batch(b, is_first, is_last):
                load_res(b)
                if there(b, 2):
                    load_in(b.step(2))
                pack_max(b, 1)
                if there(b, 1):
                    for n in range(PARTS):
                        pack_operand(sp, b.step(1), "q", n)
                        pack_operand(sp, b.step(1), "k", n)
                pack_max(b, 2)
                if not is_first:
                    store(b.step(-1))
                pack_max(b, 3)
                if there(b, 1):
                    pack_max(b.step(1), 0)

            begin = Turn(0, 0)
            load_in(begin)
            load_in(begin.step(1))
            for n in range(PARTS):
                pack_operand(sp, begin, "q", n)
            pack_max(begin, 0)
            all_batches(sp, batch)
            store(Turn(0, NB - 1))
            for par in range(2):
                sp.wait_ge(stored[par], 16 * NB // 2)

        @block.tensor
        def _(pe):
            def quad_out(b, g):
                need(pe, norm_step, b.count(NORM_STEPS * NQ, NORM_STEPS * (g + 1)))

            def turn_x(b):
                pe.wait_ge(normed, b.count(1, 1))
                quad_out(b.step(-2), 2)
                for t in range(NT):
                    last = nc.tensor.transpose(p_x[:, t * P:(t + 1) * P], xn[:, t, :], w.ident[:])
                last.then_inc(xn_turned, 1)

            def project_qk(b, o, weights):
                pe.wait_ge(xt_low_ready, b.count(1, 1))
                if o == "q":
                    need(pe, max_negated, b.count(NQ, 2 - NQ))
                else:
                    pe.wait_ge(copied["q"], b.count(1, 1))
                nc.tensor.matmul(p_x[:], weights[0][:], xt_high[:], start=True, stop=False)
                nc.tensor.matmul(p_x[:], weights[1][:], xt_high[:], start=False, stop=False)
                nc.tensor.matmul(p_x[:], weights[0][:], xt_low[:], start=False, stop=True)\
                    .then_inc(projected[o], 1)

            def project_v(b):
                pe.wait_ge(copied["k"], b.count(1, 1))
                need(pe, max_negated, b.count(NQ, 3 - NQ))
                need(pe, out_ready, b.count(1, -1))
                for t in range(NT):
                    last = nc.tensor.matmul(p_x[:, t * P:(t + 1) * P], xt[:, t * P:(t + 1) * P], w.wv[:],
                                            start=True, stop=True)
                last.then_inc(projected["v"], 1)

            def score_max(b, g, t, h):
                n = g * TILES_Q + t * QUAD + h
                need(pe, max_read, b.count(TILES_B, n + 1 - len(p_max)))
                nc.tensor.matmul(p_max[n % len(p_max)][:], pack["q"][b.par][0:MAX_ROW, g * QUAD + h, t * P:(t + 1) * P],
                                 pack["k"][b.par][0:MAX_ROW, g * QUAD + h, :], start=True, stop=True)\
                    .then_inc(max_tile, 1)

            def score_exp(b, g, t, h):
                n = g * TILES_Q + t * QUAD + h
                need(pe, exp_ready, b.count(TILES_B, n + 1 - len(p_exp)))
                rows = MAX_ROW + PARTS
                nc.tensor.matmul(p_exp[n % len(p_exp)][:], pack["k"][b.par][0:rows, g * QUAD + h, t * P:(t + 1) * P],
                                 pack["q"][b.par][0:rows, g * QUAD + h, :], start=True, stop=True)\
                    .then_inc(exp_tile, 1)

            def times_values(b, g, t):
                m = g * NT + t
                pe.wait_ge(exp_ready, b.count(TILES_B, (m + 1) * QUAD))
                if t == 0:
                    need(pe, o_copied, b.count(NQ, g))
                    pe.wait_ge(v_ready, b.count(1, 1))
                for h in range(QUAD):
                    last = nc.tensor.matmul(p_o[h * COLS:(h + 1) * COLS, :],
                                            values[b.par][:, t, g * QUAD + h, :],
                                            exps[(m * QUAD + h) % RING][:], start=t == 0, stop=t == NT - 1,
                                            tile_position=(0, h * COLS))
                last.then_inc(pv_done, 1)

            def turn_max(b, g):
                pe.wait_ge(max_read, b.count(TILES_B, (g + 1) * TILES_Q))
                if g == 0:
                    pe.wait_ge(v_ready, b.count(1, 1))
                    quad_out(b.step(-1), 1)
                elif g == 1:
                    if there(b, 1):
                        pe.wait_ge(xt_copied, b.count(1, 2))
                    else:
                        quad_out(b.step(-1), 2)
                elif g == 2:
                    if there(b, 1):
                        pe.wait_ge(copied["k"], b.count(1, 2))
                    quad_out(b.step(-1), 3)
                elif there(b, 1):
                    pe.wait_ge(v_ready, b.count(1, 2))
                else:
                    pe.wait_ge(out_ready, b.count(1))
                nc.tensor.transpose(p_x[:, 0:P], maxima[g % 2][:], w.ident[:]).then_inc(max_turned, 1)

            def turn_o(b, g):
                pe.wait_ge(o_copied, b.count(NQ, g + 1))
                if g == 0:
                    pe.wait_ge(max_negated, b.count(NQ, 4))
                elif g == 1:
                    quad_out(b, 0)
                elif g == 2:
                    quad_out(b, 1)
                    if there(b, 1):
                        pe.wait_ge(max_negated, b.count(NQ, 5))
                elif there(b, 2):
                    pe.wait_ge(copied["k"], b.count(1, 3))
                elif there(b, 1):
                    pe.wait_ge(max_negated, b.count(NQ, 6))
                else:
                    quad_out(b, 2)
                for t in range(NT):
                    last = nc.tensor.transpose(p_x[:, t * P:(t + 1) * P], o_raw[g % 2][:, t * P:(t + 1) * P],
                                               w.ident[:])
                last.then_inc(o_turned, 1)

            def turn_norm(b):
                quad_out(b, 3)
                if there(b, 1):
                    pe.wait_ge(max_negated, b.count(NQ, NQ + 3))
                for t in range(NT):
                    last = nc.tensor.transpose(p_x[:, t * P:(t + 1) * P], o_norm[:, t, :], w.ident[:])
                last.then_inc(norm_turned, 1)

            def project_out(b):
                pe.wait_ge(ot_copied, b.count(1, 1))
                for t in range(NT):
                    last = nc.tensor.matmul(p_x[:, t * P:(t + 1) * P], ot[:, t * P:(t + 1) * P], w.wo[:],
                                            start=True, stop=True)
                last.then_inc(out_projected, 1)

            def maxima_of(b, g, t):
                if g == 0 and t == 0:
                    pe.wait_ge(packed[b.par], b.half(PACK_DMA, PACK_DMA))
                for h in range(QUAD):
                    score_max(b, g, t, h)

            def batch(b, is_first, is_last):
                for g in range(NQ):
                    ahead = quad(b, g + 2)
                    for t in range(NT):
                        if t == 0:
                            pe.wait_ge(max_packed[g % 2], b.count(MAX_DMA * NQ // 2, MAX_DMA * (g // 2 + 1)))
                            if g == 2 and there(ahead[0]):
                                pe.wait_ge(packed[ahead[0].par], ahead[0].half(PACK_DMA, PACK_DMA))
                        tiles = {"M": iter(range(QUAD)), "E": iter(range(QUAD))}
                        for half, ops in enumerate(("EMEM", "MEME")):
                            for op in ops:
                                h = next(tiles[op])
                                if op == "E":
                                    score_exp(b, g, t, h)
                                elif there(ahead[0]):
                                    score_max(*ahead, t, h)
                            if half == 0:
                                pieces(b, (g, t), is_first)
                            elif t > 0:
                                times_values(b, g, t - 1)
                            elif g > 0:
                                times_values(b, g - 1, NT - 1)
                            elif not is_first:
                                times_values(b.step(-1), NQ - 1, NT - 1)

            def pieces(b, now, is_first):
                a, c = b.step(-1), b.step(1)
                if now == (0, 0):
                    turn_max(b, 1)
                if there(b, 1):
                    if now == (0, 1):
                        project_qk(c, "q", w.wq)
                    if now == (0, 2):
                        project_qk(c, "k", w.wk)
                    if now == (1, 3):
                        project_v(c)
                    if now == (3, 0):
                        turn_max(c, 0)
                if not is_first:
                    if now == (0, 3):
                        turn_o(a, 3)
                    if now == (1, 1):
                        turn_norm(a)
                    if now == (1, 2):
                        project_out(a)
                if now == (1, 0):
                    turn_max(b, 2)
                if now == (2, 0):
                    turn_max(b, 3)
                if now in ((2, 1), (2, 2), (3, 2)):
                    turn_o(b, {(2, 1): 0, (2, 2): 1, (3, 2): 2}[now])
                if now == (3, 3) and there(b, 2):
                    turn_x(b.step(2))

            begin, end = Turn(0, 0), Turn(0, NB - 1)
            turn_x(begin)
            project_qk(begin, "q", w.wq)
            project_qk(begin, "k", w.wk)
            project_v(begin)
            for g in range(2):
                for t in range(NT):
                    maxima_of(begin, g, t)
                if g == 0:
                    turn_max(begin, 0)
                    pe.wait_ge(max_negated, 1)
                    turn_x(begin.step(1))
            all_batches(pe, batch)
            times_values(end, NQ - 1, NT - 1)
            turn_o(end, NQ - 1)
            turn_norm(end)
            project_out(end)

        @block.scalar
        def _(act):
            def x_copy(b):
                act.wait_ge(xn_turned, b.count(1, 1))
                need(act, projected["v"], b.count(1))
                need(act, xt_low_ready, b.count(1))
                nc.scalar.activation(xt[:], p_x[:], ACT.Copy).then_inc(xt_copied, 1)

            def x_high(b):
                act.wait_ge(xt_copied, b.count(1, 1))
                need(act, projected["k"], b.count(1))
                nc.scalar.activation(xt_high[:], xt[:], ACT.Copy).then_inc(xt_high_ready, 1)

            def operand(b, o, bias):
                act.wait_ge(projected[o], b.count(1, 1))
                need(act, third[o], b.count(1))
                nc.scalar.activation(full[o][:], p_x[:], ACT.Identity, bias=bias[:]).then_inc(copied[o], 1)

            def operand_first(b, o):
                act.wait_ge(copied[o], b.count(1, 1))
                need(act, packed[1 - b.par], b.step(-1).half(PACK_DMA, PACK_DMA)
                     if there_before(b) else 0)
                nc.scalar.activation(parts[o][:, 0, :], full[o][:], ACT.Copy).then_inc(first[o], 1)

            def there_before(b):
                return not isinstance(b.j, int) or b.k > 0

            def operand_second(b, o):
                act.wait_ge(rested[o], b.count(1, 1))
                nc.scalar.activation(parts[o][:, 1, :], rest[o][:], ACT.Copy).then_inc(second[o], 1)

            def negate_max(b, g):
                act.wait_ge(max_turned, b.count(NQ, g + 1))
                need(act, max_step, b.count(MAX_STEPS * NQ, MAX_STEPS * g))
                nc.scalar.activation(max_neg[:], p_x[0:TILES_Q, 0:P], ACT.Copy, scale=-1.0).then_inc(max_negated, 1)

            def exponential(b, g, t, h):
                n = g * TILES_Q + t * QUAD + h
                act.wait_ge(exp_tile, b.count(TILES_B, n + 1))
                need(act, pv_done, b.count(TILES_B // QUAD, n // QUAD - 1))
                nc.scalar.activation(exps[n % RING][:], p_exp[n % len(p_exp)][:], ACT.Exp, scale=inv_sqrt)\
                    .then_inc(exp_ready, 1)

            def copy_o(b, g):
                act.wait_ge(pv_done, b.count(TILES_B // QUAD, (g + 1) * NT))
                need(act, o_turned, b.count(NQ, g - 1))
                nc.scalar.activation(o_raw[g % 2][:], p_o[:], ACT.Copy).then_inc(o_copied, 1)

            def copy_ot(b):
                act.wait_ge(norm_turned, b.count(1, 1))
                need(act, out_projected, b.count(1))
                nc.scalar.activation(ot[:], p_x[:], ACT.Copy).then_inc(ot_copied, 1)

            def batch(b, is_first, is_last):
                for g in range(NQ):
                    for t in range(NT):
                        for h in range(QUAD):
                            exponential(b, g, t, h)
                            if h % 2:
                                pieces(b, (g, t, h // 2), is_first)

            def pieces(b, now, is_first):
                a, c = b.step(-1), b.step(1)
                if now[1:] == (0, 1):
                    if now[0] < NQ - 1:
                        negate_max(b, now[0] + 1)
                    elif there(b, 1):
                        negate_max(c, 0)
                if now[1:] == (0, 1):
                    if now[0] > 0:
                        copy_o(b, now[0] - 1)
                    elif not is_first:
                        copy_o(a, NQ - 1)
                if there(b, 1):
                    if now == (0, 1, 1):
                        operand(c, "q", w.bq)
                    if now == (0, 2, 0):
                        operand_first(c, "q")
                    if now == (0, 2, 1):
                        operand(c, "k", w.bk)
                    if now == (0, 3, 0):
                        operand_first(c, "k")
                    if now == (0, 3, 1):
                        operand_second(c, "q")
                    if now == (1, 0, 0):
                        operand_second(c, "k")
                if now == (1, 1, 1) and not is_first:
                    copy_ot(a)
                if now == (3, 3, 0) and there(b, 2):
                    x_copy(b.step(2))
                if now == (3, 3, 1) and there(b, 2):
                    x_high(b.step(2))

            begin, end = Turn(0, 0), Turn(0, NB - 1)
            x_copy(begin)
            x_high(begin)
            for o, bias in (("q", w.bq), ("k", w.bk)):
                operand(begin, o, bias)
                operand_first(begin, o)
            for o in "qk":
                operand_second(begin, o)
            for n in range(PARTS):
                pack_operand(act, begin, "k", n)
            negate_max(begin, 0)
            x_copy(begin.step(1))
            x_high(begin.step(1))
            all_batches(act, batch)
            copy_o(end, NQ - 1)
            copy_ot(end)

        @block.gpsimd
        def _(pool):
            G = nc.gpsimd

            def rstd_batch(b):
                pool.wait_ge(var_ready, b.count(1, 1))
                need(pool, normed, b.count(1))
                G.tensor_tensor(norm.rstd[:], norm.var_eps[:], w.minus_half[:], ALU.pow).then_inc(rstd_ready, 1)

            def x_rest(b):
                pool.wait_ge(xt_high_ready, b.count(1, 1))
                G.tensor_tensor(xt_low[:], xt[:], xt_high[:].bitcast(F32), ALU.subtract).then_inc(xt_low_ready, 1)

            def operand_rest(b, o):
                pool.wait_ge(first[o], b.count(1, 1))
                G.tensor_tensor(rest[o][:], full[o][:], parts[o][:, 0, :], ALU.subtract).then_inc(rested[o], 1)

            def operand_third(b, o):
                pool.wait_ge(second[o], b.count(1, 1))
                G.tensor_tensor(parts[o][:, 2, :], rest[o][:], parts[o][:, 1, :], ALU.subtract).then_inc(third[o], 1)

            def split_max(b, g):
                out = max_parts[g % 2]
                at = lambda n: b.count(MAX_STEPS * NQ, MAX_STEPS * g + n)
                pool.wait_ge(max_negated, b.count(NQ, g + 1))
                need(pool, max_packed[g % 2], b.count(MAX_DMA * NQ // 2, MAX_DMA * (g // 2)))
                G.tensor_tensor(out[:, 0, :], max_neg[:], zeros[:], ALU.add).then_inc(max_step, 1)
                pool.wait_ge(max_step, at(1))
                G.tensor_tensor(max_rest[:], max_neg[:], out[:, 0, :], ALU.subtract).then_inc(max_step, 1)
                pool.wait_ge(max_step, at(2))
                G.tensor_tensor(out[:, 1, :], max_rest[:], zeros[:], ALU.add).then_inc(max_step, 1)
                pool.wait_ge(max_step, at(3))
                G.tensor_tensor(out[:, 2, :], max_rest[:], out[:, 1, :], ALU.subtract).then_inc(max_step, 1)

            def add_bias(b):
                pool.wait_ge(x_res_loaded[b.par], b.half(16, 16))
                need(pool, out_ready, b.count(1))
                G.tensor_tensor(x_bias[:], x_res[b.par][:], w.bo[:].unsqueeze(1).to_broadcast([P, NT, D]),
                                ALU.add).then_inc(bias_ready, 1)

            def batch(b, is_first, is_last):
                c = b.step(1)
                split_max(b, 1)
                if there(b, 2):
                    rstd_batch(b.step(2))
                if there(b, 1):
                    for part in (operand_rest, operand_third):
                        part(c, "q")
                        part(c, "k")
                split_max(b, 2)
                add_bias(b)
                split_max(b, 3)
                if there(b, 1):
                    split_max(c, 0)
                if there(b, 2):
                    x_rest(b.step(2))

            begin = Turn(0, 0)
            rstd_batch(begin)
            x_rest(begin)
            rstd_batch(begin.step(1))
            for part in (operand_rest, operand_third):
                part(begin, "q")
                part(begin, "k")
            split_max(begin, 0)
            x_rest(begin.step(1))
            all_batches(pool, batch)

        @block.vector
        def _(dve):
            V = nc.vector

            norm_stats, norm_var, norm_apply = normalisation(
                nc, dve, x_in, xn, norm, x_in_loaded, stats_done, var_ready, rstd_ready, normed, xn_turned)

            def take_max(b, g, t, h):
                n = g * TILES_Q + t * QUAD + h
                dve.wait_ge(max_tile, b.count(TILES_B, n + 1))
                if t == 0 and h == 0:
                    need(dve, max_turned, b.count(NQ, g - 1))
                V.tensor_reduce(maxima[g % 2][:, h * NT + t:h * NT + t + 1], p_max[n % len(p_max)][:],
                                AX.X, ALU.max).then_inc(max_read, 1)

            def copy_values(b):
                dve.wait_ge(projected["v"], b.count(1, 1))
                need(dve, pv_done, b.count(TILES_B // QUAD, -TILES_B // QUAD))
                V.tensor_tensor(values[b.par][:, :, :, 0:HD],
                                p_x[:].rearrange("p (t h d) -> p t h d", t=NT, d=HD),
                                w.bv[:].rearrange("p (h d) -> p h d", d=HD).unsqueeze(1)
                                .to_broadcast([P, NT, HEADS, HD]), ALU.add).then_inc(v_ready, 1)

            def normalise(b, g):
                at = lambda n: b.count(NORM_STEPS * NQ, NORM_STEPS * g + n)
                quads = p_x[:].rearrange("p (t h c) -> p t h c", t=NT, c=COLS)
                dve.wait_ge(o_turned, b.count(NQ, g + 1))
                V.reciprocal(sums_inv[:], quads[:, :, :, HD]).then_inc(norm_step, 1)
                dve.wait_ge(norm_step, at(1))
                V.tensor_tensor(sums_scale[:], sums_inv[:], w.head_mask[:, g * QUAD:(g + 1) * QUAD]
                                .unsqueeze(1).to_broadcast([P, NT, QUAD]), ALU.mult).then_inc(norm_step, 1)
                dve.wait_ge(norm_step, at(2))
                need(dve, norm_turned, b.count(1))
                out = o_norm[:, :, g * QUAD * HD:(g + 1) * QUAD * HD].rearrange("p t (h d) -> p t h d", d=HD)
                V.tensor_tensor(out, quads[:, :, :, 0:HD], sums_scale[:].unsqueeze(3)
                                .to_broadcast([P, NT, QUAD, HD]), ALU.mult).then_inc(norm_step, 1)

            def residual(b):
                dve.wait_ge(out_projected, b.count(1, 1))
                dve.wait_ge(bias_ready, b.count(1, 1))
                need(dve, stored[b.par], b.half(16))
                V.tensor_tensor(x_out[b.par][:], p_x[:].rearrange("p (t d) -> p t d", d=D), x_bias[:],
                                ALU.add).then_inc(out_ready, 1)

            def batch(b, is_first, is_last):
                for g in range(NQ):
                    ahead = quad(b, g + 2)
                    for t in range(NT):
                        for h in range(QUAD):
                            if there(ahead[0]):
                                take_max(*ahead, t, h)
                            if h % 2:
                                pieces(b, (g, t, h // 2), is_first)

            def pieces(b, now, is_first):
                a, c = b.step(-1), b.step(1)
                if not is_first:
                    if now == (0, 3, 0):
                        normalise(a, NQ - 1)
                    if now == (1, 2, 0):
                        residual(a)
                if now == (1, 3, 0) and there(b, 1):
                    copy_values(c)
                if now in ((2, 1, 0), (2, 2, 0), (3, 2, 0)):
                    normalise(b, {(2, 1, 0): 0, (2, 2, 0): 1, (3, 2, 0): 2}[now])
                if there(b, 2):
                    if now == (0, 1, 0):
                        norm_stats(b.step(2))
                    if now == (0, 1, 1):
                        norm_var(b.step(2))
                    if now == (1, 0, 1):
                        norm_apply(b.step(2))

            begin, end = Turn(0, 0), Turn(0, NB - 1)
            for n in range(2):
                norm_stats(begin.step(n))
                norm_var(begin.step(n))
                norm_apply(begin.step(n))
            copy_values(begin)
            for g in range(2):
                for t in range(NT):
                    for h in range(QUAD):
                        take_max(begin, g, t, h)
            all_batches(dve, batch)
            normalise(end, NQ - 1)
            residual(end)


class Weights:

    def __init__(self, nc, ctx):
        sb = lambda name, shape, dt=F32: ctx.enter_context(nc.sbuf_tensor(name, shape, dt))
        both = lambda name, shape: [sb(f"{name}_high", shape, F32R), sb(f"{name}_low", shape, F32R)]
        self.gate, self.up = both("gate", [P, HID]), both("up", [P, HID])
        self.down = both("down", [P, TILES, D])
        self.wq, self.wk = both("wq", [P, D]), both("wk", [P, D])
        self.wv, self.wo = sb("wv", [P, D]), sb("wo", [P, D])
        self.bq, self.bk, self.bv, self.bo = sb("bq", [P, 1]), sb("bk", [P, 1]), sb("bv", [P, D]), sb("bo", [P, D])
        self.head_mask, self.gate_w = sb("head_mask", [P, HEADS]), sb("gate_w", [P, E])
        self.rank = sb("rank", [P, NT, E])
        self.ident, self.ident16 = sb("ident", [P, P]), sb("ident16", [P, P], BF16)
        self.selector = sb("selector", [P, ROUTED], BF16)
        self.minus_half = sb("minus_half", [P, NT])
        self.pack = {o: [sb(f"{o}_pack{i}", [P, HEADS, S], BF16) for i in range(2)] for o in "qk"}
        self.values = [sb(f"values{i}", [P, NT, HEADS, COLS]) for i in range(2)]
        self.maxima = [sb(f"maxima{i}", [P, P]) for i in range(2)]
        self.zeros = sb("zeros", [TILES_Q, P])


def program(nc, dram, out):
    after_ffn = nc.dram_tensor("after_ffn", [NB * S, D], F32, kind="Internal").ap()
    after_attn = nc.dram_tensor("after_attn", [NB * S, D], F32, kind="Internal").ap()
    with ExitStack() as ctx:
        w = Weights(nc, ctx)
        setup(nc, dram, w)
        x = dram["x"].rearrange("b s d -> (b s) d")
        y = out.rearrange("b s d -> (b s) d")
        ffn(nc, "ffn1", w, x, after_ffn)
        attention(nc, w, after_ffn, after_attn)
        ffn(nc, "ffn2", w, after_attn, y)


def kernel(**inputs):
    import numpy as np
    import concourse.bacc as bacc
    from concourse.bass_utils import run_bass_kernel_spmd

    data = {k.replace("L0_attn_", "").replace("L0_ffn_", ""): np.asarray(v) for k, v in inputs.items()}
    arrays = {k: data[k] for k in ("x", "bq", "bk", "bv", "bo", "head_mask", "w_gate", "w_up", "w_down",
                                   "sw_gate", "sw_up", "sw_down")}
    by_d = lambda a: a.reshape(-1, HEADS, HD).swapaxes(1, 2).reshape(a.shape)
    arrays |= {"bq": by_d(data["bq"]), "bk": by_d(data["bk"])}
    arrays |= {"wq_t": by_d(data["Wq"].T), "wk_t": by_d(data["Wk"].T), "wv_t": data["Wv"].T, "wo_t": data["Wo"].T,
               "gate_w_t": data["gate_w"].T}
    arrays["identity"] = np.eye(P, dtype=np.float32)
    arrays["rank"] = np.ascontiguousarray(np.broadcast_to(np.arange(E, 0, -1, dtype=np.float32), (P, NT, E)))
    expert = np.arange(ROUTED) // F
    arrays["selector"] = (np.arange(PARTS * E)[:, None] % E == expert[None, :]).astype(np.float32)
    arrays = {f"in_{k}": np.ascontiguousarray(a) for k, a in arrays.items()}

    nc = bacc.Bacc("TRN2", target_bir_lowering=False, num_devices=1)
    dram = {k[3:]: nc.dram_tensor(k, a.shape, mybir.dt.from_np(a.dtype), kind="ExternalInput").ap()
            for k, a in arrays.items()}
    out = nc.dram_tensor("out", (NB, S, D), F32, kind="ExternalOutput").ap()
    program(nc, dram, out)
    result = run_bass_kernel_spmd(nc, [arrays], core_ids=[0])
    return result.results[0]["out"]
```
